# Optimizing a Trainium2 kernel written in Bass

```python
import numpy as np
import jax
import jax.numpy as jnp

def _softmax(x, axis=-1):
    return jax.nn.softmax(x, axis=axis)

def _gelu(x):
    return jax.nn.gelu(x, approximate=True)

def _silu(x):
    return jax.nn.silu(x)

def _sigmoid(x):
    return jax.nn.sigmoid(x)

def _layernorm(x, axis=-1, eps=1e-05):
    m = jnp.mean(x, axis=axis, keepdims=True)
    v = jnp.var(x, axis=axis, keepdims=True)
    return (x - m) / jnp.sqrt(v + eps)

def _scatter_add(tgt, idx, src, axis=0):
    return tgt.at[idx].add(src)

def _segment_sum(src, seg, n):
    return jax.ops.segment_sum(src, seg, n)
kernel_name = 'mk_adj_preln_d2_adj_r2_24ec30'

def setup_inputs(seed: int=0):
    np.random.seed(seed)
    _w = jnp.asarray

    def _rec_inputs():
        import jax
        import jax.numpy as jnp
        _gk = jax.random.key(seed)
        x = -0.000929 + 1 * jax.random.normal(jax.random.fold_in(_gk, 1), (8192, 64), jnp.float32)
        _w = (1.0 + jnp.arange(8192, dtype=jnp.float32)) ** (-0.5)
        _w = _w / _w.mean()
        _pij = jnp.clip(0.000244141 * _w[:, None] * _w[None, :], 0.0, 1.0)
        _a = jax.random.uniform(jax.random.fold_in(_gk, 2), (8192, 8192)) < _pij
        _a = jnp.logical_or(_a, jnp.eye(8192, dtype=bool))
        _af = _a.astype(jnp.float32)
        _af = _af * jax.random.uniform(jax.random.fold_in(_gk, 3), (8192, 8192), jnp.float32, 0.05, 1)
        adj = _af
        return (x, adj)
    x, adj = _rec_inputs()

    def _L0_gnn_setup():
        import jax, jax.numpy as jnp
        import numpy as np
        N, D, H = (8192, 64, 128)
        GAIN = 0.2
        key = jax.random.key(seed)
        ks = jax.random.split(key, 6)
        X = jax.random.normal(ks[0], (N, D), dtype=jnp.float32)
        t = jax.random.uniform(ks[1], (1,), dtype=jnp.float32)
        Wt = jax.random.uniform(ks[2], (N, N), dtype=jnp.float32)
        B = GAIN * jnp.eye(D, dtype=jnp.float32) + 0.01 * jax.random.normal(ks[3], (D, D), dtype=jnp.float32)
        W1 = jax.random.normal(ks[4], (D + 1, H), dtype=jnp.float32) * (1.0 / np.sqrt(D + 1))
        b1 = jnp.zeros((H,), dtype=jnp.float32)
        W2 = jax.random.normal(ks[5], (H, D), dtype=jnp.float32) * (1.0 / np.sqrt(H))
        b2 = jnp.zeros((D,), dtype=jnp.float32)
        return {'X': X, 't': t, 'Wt': Wt, 'B': B, 'W1': W1, 'b1': b1, 'W2': W2, 'b2': b2}
    _L0_gnn_all = _L0_gnn_setup()
    _L0_gnn_in = {k: v for k, v in _L0_gnn_all.items() if k in ('t', 'B', 'W1', 'b1', 'W2', 'b2')}
    del _L0_gnn_all

    def _L1_gnn_setup():
        import jax, jax.numpy as jnp
        import numpy as np
        N = 2048
        F = 64
        H = 8
        D = 8
        key = jax.random.key(seed)
        k1, k2, k3, k4, k5, k6 = jax.random.split(key, 6)
        X = jax.random.normal(k1, (N, F), dtype=jnp.float32)
        A = (jax.random.uniform(k2, (N, N)) < 0.01).astype(jnp.float32)
        A = jnp.maximum(A, jnp.eye(N, dtype=jnp.float32))
        lim_w = np.sqrt(6.0 / (F + H * D)).astype(np.float32)
        W = jax.random.uniform(k3, (F, H * D), minval=-lim_w, maxval=lim_w, dtype=jnp.float32)
        lim_a = np.sqrt(6.0 / (1 + H * D)).astype(np.float32)
        att_self = jax.random.uniform(k4, (H, D), minval=-lim_a, maxval=lim_a, dtype=jnp.float32)
        att_neigh = jax.random.uniform(k5, (H, D), minval=-lim_a, maxval=lim_a, dtype=jnp.float32)
        bias = jnp.zeros((H, D), dtype=jnp.float32)
        return {'X': X, 'A': A, 'W': W, 'att_self': att_self, 'att_neigh': att_neigh, 'bias': bias}
    _L1_gnn_all = _L1_gnn_setup()
    _L1_gnn_in = {k: v for k, v in _L1_gnn_all.items() if k in ('W', 'att_self', 'att_neigh', 'bias')}
    del _L1_gnn_all
    return {'x': x, 'adj': adj, 'L0_gnn_t': _L0_gnn_in['t'], 'L0_gnn_B': _L0_gnn_in['B'], 'L0_gnn_W1': _L0_gnn_in['W1'], 'L0_gnn_b1': _L0_gnn_in['b1'], 'L0_gnn_W2': _L0_gnn_in['W2'], 'L0_gnn_b2': _L0_gnn_in['b2'], 'L1_gnn_W': _L1_gnn_in['W'], 'L1_gnn_att_self': _L1_gnn_in['att_self'], 'L1_gnn_att_neigh': _L1_gnn_in['att_neigh'], 'L1_gnn_bias': _L1_gnn_in['bias']}

def reference(x, adj, L0_gnn_t, L0_gnn_B, L0_gnn_W1, L0_gnn_b1, L0_gnn_W2, L0_gnn_b2, L1_gnn_W, L1_gnn_att_self, L1_gnn_att_neigh, L1_gnn_bias):
    import jax
    import jax.numpy as jnp

    def _L0_gnn_ref(X, t, Wt, B, W1, b1, W2, b2):
        import jax, jax.numpy as jnp
        import numpy as np
        N, D, H = (8192, 64, 128)
        GAIN = 0.2
        n = X.shape[0]
        tcol = jnp.broadcast_to(t.reshape(1, 1), (n, 1))
        h = jnp.tanh(jnp.concatenate([X, tcol], axis=1) @ W1 + b1)
        u_intra = h @ W2 + b2
        XB = X @ B.T
        u_comm = Wt @ XB - jnp.sum(Wt, axis=1, keepdims=True) * XB
        return u_intra + u_comm

    def _L1_gnn_ref(X, A, W, att_self, att_neigh, bias):
        import jax, jax.numpy as jnp
        import numpy as np
        N = 2048
        F = 64
        H = 8
        D = 8
        feats = (X @ W).reshape(-1, H, D)
        a_self = jnp.einsum('nhd,hd->nh', feats, att_self)
        a_neigh = jnp.einsum('nhd,hd->nh', feats, att_neigh)
        scores = a_self.T[:, :, None] + a_neigh.T[:, None, :]
        scores = jax.nn.leaky_relu(scores, negative_slope=0.2)
        scores = scores + (-10000000000.0 * (1.0 - A))[None, :, :]
        attn = jax.nn.softmax(scores, axis=-1)
        out = jnp.einsum('hij,jhd->ihd', attn, feats)
        out = out + bias[None, :, :]
        out = out.reshape(-1, H * D)
        return jax.nn.relu(out)
    h = jnp.maximum(_layernorm(x, axis=-1), 0.0)
    x = x + _L0_gnn_ref(h, L0_gnn_t, adj, L0_gnn_B, L0_gnn_W1, L0_gnn_b1, L0_gnn_W2, L0_gnn_b2)
    h = jnp.maximum(_layernorm(x, axis=-1), 0.0)
    x = x + _L1_gnn_ref(h, adj, L1_gnn_W, L1_gnn_att_self, L1_gnn_att_neigh, L1_gnn_bias)
    return x

_drawn_inputs = setup_inputs


def setup_inputs(seed=0):
    import zlib

    import numpy as np

    out = dict(_drawn_inputs(seed))
    spreads = {'L0_gnn_b1': (0.0, 0.1), 'L0_gnn_b2': (0.0, 0.1), 'L1_gnn_bias': (0.0, 0.1)}
    factors = {}
    for name, (base, spread) in spreads.items():
        noise = np.random.default_rng([zlib.crc32(name.encode()), seed]).standard_normal(out[name].shape)
        drawn = base * np.exp(spread * noise) if base else spread * noise
        out[name] = jnp.asarray(drawn.astype(out[name].dtype))
    for name, factor in factors.items():
        out[name] = (out[name] * factor).astype(out[name].dtype)
    return out
```

```python
from contextlib import ExitStack

import concourse.bass as bass
from concourse import mybir

F32 = mybir.dt.float32
I32 = mybir.dt.int32
U32 = mybir.dt.uint32
ALU = mybir.AluOpType
ACT = mybir.ActivationFunctionType
AX = mybir.AxisListType

P = 128
N = 8192
D = 64
HID = 128
HEADS, HD = 8, 8
NB = N // P
W = 512
S = N // W
TB = W // P
CB = 8
NC = NB // CB
RING = 4
HALF = CB * W // 2
FA = D + 2 * HEADS
EPS = 1e-5
SLOPE = 0.2
MASK = 1e10
LEAD = 505.0
HALF_SCORE = 50.0
OG = 8
QG = NB // OG


def build(nc, x, adj, adj_t, w1, w1_t, b1, t_in, w2, b2, b_t, w_gat, w_gat_t, att_self, att_neigh, bias, out):
    with ExitStack() as ctx:
        def sb(name, shape, dt=F32):
            return ctx.enter_context(nc.sbuf_tensor(name, shape, dt))

        def pb(name, shape, dt=F32):
            return ctx.enter_context(nc.psum_tensor(name, shape, dt))

        def sem(name):
            return ctx.enter_context(nc.semaphore(name))

        feats_dram = nc.dram_tensor("feats_dram", (N, D), F32, kind="Internal").ap()
        neigh_dram = nc.dram_tensor("neigh_dram", (HEADS, N), F32, kind="Internal").ap()

        ring = sb("ring", [P, RING * CB * W])
        xb_ones = sb("xb_ones", [P, NB, D + 1])
        h_t = sb("h_t", [P, N])
        x_pb = sb("x_pb", [P, NB, D])
        x_tq = sb("x_tq", [P, NB, D])
        feats = sb("feats", [P, NB * FA])
        max_lo = sb("max_lo", [P, HALF])
        max_hi = sb("max_hi", [P, HALF])
        cand = sb("cand", [P, TB, NB])
        hidden = sb("hidden", [HID, W])
        acc_sb = sb("acc_sb", [D + 1, W])
        acc_tq = sb("acc_tq", [P, TB, D + 1])
        tmp = sb("tmp", [P, TB, D])
        cen = sb("cen", [P, TB, D])
        h1 = sb("h1", [P, TB, D])
        h1_t = sb("h1_t", [D, W])
        h_strip = sb("h_strip", [D, W])
        stat = sb("stat", [P, 4, TB])
        rstd = sb("rstd", [P, TB])
        squares = sb("squares", [P, CB, D])
        pstat = sb("pstat", [P, 5, NB])
        ident = sb("ident", [P, P])
        b_t_sb = sb("b_t_sb", [D, D])
        w1_sb = sb("w1_sb", [D, HID])
        w2_sb = sb("w2_sb", [HID, D + 1])
        hid_bias = sb("hid_bias", [HID, 4])
        out_bias = sb("out_bias", [D + 1, 1])
        w_ext = sb("w_ext", [D, FA])
        w_gat_t_sb = sb("w_gat_t_sb", [D, D])
        att_diag = sb("att_diag", [D, 2 * HEADS])
        att_col = sb("att_col", [D, 2])
        head_mask = sb("head_mask", [D, HEADS])
        bias_row = sb("bias_row", [P, D])
        eps = sb("eps", [P, 1])
        ones = sb("ones", [P, 1])
        row_base = sb("row_base", [P, NB], I32)
        runmax = sb("runmax", [P, W])
        top_cls = sb("top_cls", [P, TB, 8])
        idx_cls = sb("idx_cls", [P, TB, 8], U32)
        top_cand = sb("top_cand", [P, TB, 8])
        idx_cand = sb("idx_cand", [P, TB, 8], U32)
        cls_row = sb("cls_row", [P, TB], U32)
        first = sb("first", [P, NB])
        second = sb("second", [P, NB])
        best = sb("best", [P, NB], U32)
        score_max = sb("score_max", [P, S])
        gap = sb("gap", [P, 4, NB])
        good = sb("good", [P, 4])
        flag = sb("flag", [1, 1], I32)
        gathered = x_pb

        acc = [pb(f"acc{i}", [P, W]) for i in range(2)]
        ps_hid = pb("ps_hid", [P, W])
        ps_acc = pb("ps_acc", [P, TB, D + 1])
        ps_xb = pb("ps_xb", [P, TB, D])
        ps_h = pb("ps_h", [P, W])
        ps_max = pb("ps_max", [P, W])
        ps_feat = pb("ps_feat", [P, TB, FA])

        consts_in = sem("consts_in")
        att_in = sem("att_in")
        x_in = sem("x_in")
        x_tq_in = sem("x_tq_in")
        w_in = sem("w_in")
        pool_const = sem("pool_const")
        dve_const = sem("dve_const")
        w_ext_ready = sem("w_ext_ready")
        w_ext_done = sem("w_ext_done")
        pro_chain = sem("pro_chain")
        pro_var = sem("pro_var")
        pro_std = sem("pro_std")
        pro_norm = sem("pro_norm")
        pro_turned = sem("pro_turned")
        pro_h = sem("pro_h")
        pro_xb = sem("pro_xb")
        xb_done = sem("xb_done")
        chunk_in = [sem(f"chunk_in{r}") for r in range(RING)]
        pe_chunk = sem("pe_chunk")
        lo_done = sem("lo_done")
        hi_done = sem("hi_done")
        fold = sem("fold")
        hid_ready = sem("hid_ready")
        hid_done = sem("hid_done")
        strip_h_done = sem("strip_h_done")
        acc_ready = sem("acc_ready")
        acc_copied = sem("acc_copied")
        acc_turned = sem("acc_turned")
        acc_tq_done = sem("acc_tq_done")
        chain = sem("chain")
        x1_done = sem("x1_done")
        var_done = sem("var_done")
        std_done = sem("std_done")
        h1_done = sem("h1_done")
        h1_turned = sem("h1_turned")
        h1_t_done = sem("h1_t_done")
        feat_ready = sem("feat_ready")
        feat_done = sem("feat_done")
        feat_stored = sem("feat_stored")
        score_done = sem("score_done")
        runmax_done = sem("runmax_done")
        runmax_turned = sem("runmax_turned")
        cls_top = sem("cls_top")
        cls_done = sem("cls_done")
        cls_row_done = sem("cls_row_done")
        cand_in = sem("cand_in")
        cand_top = sem("cand_top")
        cand_done = sem("cand_done")
        top_kept = sem("top_kept")
        best_done = sem("best_done")
        got = [sem(f"got{g}") for g in range(QG)]
        end_chain = sem("end_chain")
        good_done = sem("good_done")
        good_count = sem("good_count")
        flag_done = sem("flag_done")
        biased = sem("biased")
        rectified = sem("rectified")
        out_done = sem("out_done")
        stored = sem("stored")
        sp_past = sem("sp_past")
        pool_past = sem("pool_past")
        dve_past = sem("dve_past")
        pe_past = sem("pe_past")
        gen_turned = sem("gen_turned")
        gen_copied = sem("gen_copied")
        gen_neigh_stored = sem("gen_neigh_stored")
        gen_row_in = sem("gen_row_in")
        gen_neigh_in = sem("gen_neigh_in")
        gen_chain = sem("gen_chain")
        gen_mask = sem("gen_mask")
        gen_max = sem("gen_max")
        gen_exp = sem("gen_exp")
        gen_p_turned = sem("gen_p_turned")
        gen_p_copied = sem("gen_p_copied")
        gen_sum = sem("gen_sum")
        gen_head = sem("gen_head")
        gen_out = sem("gen_out")
        gen_stored = sem("gen_stored")

        x_by_p = x.rearrange("(p b) d -> p b d", b=NB)
        x_by_q = x.rearrange("(t q) d -> q t d", q=P)
        out_by_q = out.rearrange("(t q) d -> q t d", q=P)
        feats_by_q = feats_dram.rearrange("(t q) d -> q t d", q=P)
        classes = adj.rearrange("i (p b) -> (i p) b", b=NB)
        h_by_block = h_t[0:D, :].rearrange("d (p b) -> d b p", b=NB)
        feats_v = feats[:, :].rearrange("q (t f) -> q t f", f=FA)
        psh = ps_h[0:D, :].rearrange("d (k q) -> d k q", q=P)
        psr_h = ps_max[0:D, :].rearrange("d (k q) -> d k q", q=P)

        def slot(n):
            return ring[:, (n % RING) * CB * W:(n % RING + 1) * CB * W]

        def wide(a, k, n=D):
            return a.unsqueeze(2).to_broadcast([P, k, n])

        block = ctx.enter_context(nc.Block())

        @block.sync
        def _(sp):
            sp.dma_start(x_pb[:, :, :], x_by_p).then_inc(x_in, 16)
            for dst, src in ((b_t_sb[:, :], b_t), (w1_sb[:, :], w1), (w2_sb[:, 0:D], w2),
                             (hid_bias[:, 0:1], b1), (hid_bias[:, 1:2], w1_t),
                             (hid_bias[:, 2:3], t_in.to_broadcast([HID, 1])), (out_bias[0:D, :], b2),
                             (w_ext[:, 0:D], w_gat), (w_gat_t_sb[:, :], w_gat_t),
                             (bias_row[:, :], bias.to_broadcast([P, D]))):
                sp.dma_start(dst, src).then_inc(consts_in, 16)
            sp.dma_start(att_col[:, 0:1], att_self).then_inc(att_in, 16)
            sp.dma_start(att_col[:, 1:2], att_neigh).then_inc(att_in, 16)
            for n in range(RING):
                sp.dma_start(slot(n), adj_t[n]).then_inc(chunk_in[n % RING], 16)
            sp.dma_start(x_tq[:, :, :], x_by_q).then_inc(x_tq_in, 16)

            def load(s, c):
                sp.wait_ge(pe_chunk, s * NC + (c - RING + 1))
                sp.wait_ge(hi_done, s * NC + (c - RING + 1))
                sp.sem_inc(sp_past, 1)
                src = adj_t[bass.ds(s * NC + c, 1)].rearrange("a p f -> (a p) f")
                sp.dma_start(slot(c), src).then_inc(chunk_in[c % RING], 16)

            def store_feats(s):
                sp.wait_ge(feat_done, s + 1)
                sp.sem_inc(sp_past, 1)
                sp.dma_start(feats_by_q[:, bass.ds(s * TB, TB), :],
                             feats_v[:, bass.ds(s * TB, TB), 0:D]).then_inc(feat_stored, 16)

            for c in range(RING, NC):
                load(0, c)
            with sp.Fori(1, S) as s:
                for c in range(NC):
                    load(s, c)
                store_feats(s - 1)
            store_feats(S - 1)
            for g in range(QG):
                sp.wait_ge(out_done, g + 1)
                ts = slice(g * OG, (g + 1) * OG)
                sp.dma_start(out_by_q[:, ts, :], gathered[:, ts, :]).then_inc(stored, 16)
            sp.wait_ge(stored, 16 * QG)

            sp.wait_ge(flag_done, 1)
            general = sp.value_load(flag[0:1, 0:1], min_val=0, max_val=1)
            with sp.If(general != 0):
                sp.wait_ge(gen_copied, NB // 4)
                sp.dma_start(neigh_dram, h_t[0:HEADS, :]).then_inc(gen_neigh_stored, 16)
                sp.wait_ge(gen_neigh_stored, 16)
                with sp.Fori(0, NB) as ib:
                    sp.wait_ge(gen_head, ib * HEADS + 1)
                    sp.sem_inc(sp_past, 1)
                    rows = adj.rearrange("(t q) j -> t q j", q=P)[bass.ds(ib, 1)]
                    sp.dma_start(ring[:, 0:N], rows.rearrange("a q j -> (a q) j")).then_inc(gen_row_in, 16)
                    with sp.Fori(0, HEADS) as h:
                        sp.wait_ge(gen_head, ib * HEADS + h + 1)
                        sp.sem_inc(sp_past, 1)
                        sp.dma_start(ring[:, N:2 * N], neigh_dram[bass.ds(h, 1), :].to_broadcast([P, N]))\
                            .then_inc(gen_neigh_in, 16)
                    sp.wait_ge(gen_out, ib + 1)
                    sp.sem_inc(sp_past, 1)
                    dst = out.rearrange("(t q) d -> t q d", q=P)[bass.ds(ib, 1)]
                    sp.dma_start(dst.rearrange("a q d -> (a q) d"), tmp[:, 0, :]).then_inc(gen_stored, 16)
                    sp.wait_ge(gen_stored, ib * 16 + 16)
                    sp.sem_inc(sp_past, 1)

        @block.gpsimd
        def _(pool):
            for n, (dst, value) in enumerate(((ones[:, :], 1.0), (eps[:, :], EPS), (xb_ones[:, :, D:D + 1], 1.0),
                                              (w2_sb[:, D:D + 1], 0.0), (out_bias[D:D + 1, :], 0.0),
                                              (head_mask[:, :], 1.0), (ident[:, :], 0.0))):
                pool.memset(dst, value).then_inc(pool_const, 1)
                pool.wait_ge(pool_const, n + 1)
            pool.affine_select(out=ident[:, :], in_=ident[:, :], compare_op=ALU.not_equal, fill=1.0,
                               base=0, pattern=[[-1, P]], channel_multiplier=1).then_inc(pool_const, 1)
            pool.wait_ge(pool_const, 8)
            pool.affine_select(out=head_mask[:, :], in_=head_mask[:, :], compare_op=ALU.is_ge, fill=0.0,
                               base=0, pattern=[[-HD, HEADS]], channel_multiplier=1).then_inc(pool_const, 1)
            pool.wait_ge(pool_const, 9)
            pool.affine_select(out=head_mask[:, :], in_=head_mask[:, :], compare_op=ALU.is_ge, fill=0.0,
                               base=HD - 1, pattern=[[HD, HEADS]], channel_multiplier=-1)\
                .then_inc(pool_const, 1)
            pool.wait_ge(pool_const, 10)
            pool.iota(row_base[:, :], pattern=[[P * P, NB]], base=0, channel_multiplier=P)\
                .then_inc(pool_const, 1)

            with pool.Fori(0, S) as s:
                pool.wait_ge(cls_row_done, s + 1)
                pool.sem_inc(pool_past, 1)
                for k in range(TB):
                    pool.indirect_dma_start(
                        out=cand[:, k, :], out_offset=None, in_=classes,
                        in_offset=bass.IndirectOffsetOnAxis(ap=cls_row[:, k:k + 1], axis=0),
                    ).then_inc(cand_in, 16)
            pool.wait_ge(best_done, S)
            pool.wait_ge(feat_stored, 16 * S)
            for t in range(NB):
                pool.indirect_dma_start(
                    out=gathered[:, t, :], out_offset=None, in_=feats_dram,
                    in_offset=bass.IndirectOffsetOnAxis(ap=best[:, t:t + 1], axis=0),
                ).then_inc(got[t // OG], 16)

        @block.scalar
        def _(act):
            act.wait_ge(pool_const, 11)
            act.wait_ge(w_ext_ready, 1)
            act.copy(w_ext[:, D:FA], ps_feat[0:D, 0, 0:2 * HEADS]).then_inc(w_ext_done, 1)

            def deviation(g):
                act.wait_ge(pro_var, g + 1)
                act.activation(pstat[:, 3, g * CB:(g + 1) * CB], pstat[:, 2, g * CB:(g + 1) * CB], ACT.Sqrt,
                               bias=eps[:, :], scale=1.0 / D).then_inc(pro_std, 1)

            def place(g):
                act.wait_ge(pro_turned, g + 1)
                for half, src in enumerate((psh, psr_h)):
                    b = g * CB + half * 4
                    act.activation(h_by_block[:, b:b + 4, :], src, ACT.Relu).then_inc(pro_h, 1)
                act.wait_ge(pro_xb, g + 1)
                act.copy(xb_ones[:, g * CB:(g + 1) * CB, 0:D],
                         ps_hid[:, :].rearrange("p (b d) -> p b d", d=D)).then_inc(xb_done, 1)

            for g in range(NC):
                deviation(g)
                if g:
                    place(g - 1)
            place(NC - 1)

            def tanh(s):
                act.wait_ge(hid_ready, s + 1)
                act.activation(hidden[:, :], ps_hid[:, :], ACT.Tanh, bias=hid_bias[:, 3:4])\
                    .then_inc(hid_done, 1)

            def strip_h(s):
                act.copy(h_strip[:, :], h_t[0:D, bass.ds(s * W, W)]).then_inc(strip_h_done, 1)

            def finish_strip(s, parity, last=False):
                act.wait_ge(acc_ready, s + 1)
                act.activation(acc_sb[:, :], acc[parity][0:D + 1, :], ACT.Identity, bias=out_bias[:, :])\
                    .then_inc(acc_copied, 1)
                act.wait_ge(acc_turned, s + 1)
                act.copy(acc_tq[:, :, :], ps_acc[:, :, :]).then_inc(acc_tq_done, 1)
                if not last:
                    strip_h(s + 1)
                act.wait_ge(var_done, s + 1)
                act.activation(stat[:, 3, :], stat[:, 2, :], ACT.Sqrt, bias=eps[:, :], scale=1.0 / D)\
                    .then_inc(std_done, 1)
                act.wait_ge(h1_turned, s + 1)
                act.activation(h1_t[:, :], ps_h[0:D, :], ACT.Relu).then_inc(h1_t_done, 1)
                act.wait_ge(feat_ready, s + 1)
                act.copy(feats[:, bass.ds(s * (TB * FA), TB * FA)],
                         ps_feat[:, :, :].rearrange("q t f -> q (t f)")).then_inc(feat_done, 1)

            strip_h(0)
            act.wait_ge(dve_const, 4)
            tanh(0)
            with act.Fori(0, S // 2 - 1) as r:
                for k in range(2):
                    finish_strip(2 * r + k, k)
                    tanh(2 * r + k + 1)
            finish_strip(S - 2, 0)
            tanh(S - 1)
            finish_strip(S - 1, 1, last=True)

            act.wait_ge(flag_done, 1)
            general = act.value_load(flag[0:1, 0:1], min_val=0, max_val=1)
            with act.If(general != 0):
                with act.Fori(0, NB * HEADS) as n:
                    act.wait_ge(gen_max, n + 1)
                    act.activation(h_t[:, :], h_t[:, :], ACT.Exp, bias=gap[:, 1, 0:1], accum_out=gap[:, 2, 0:1])\
                        .then_inc(gen_exp, 1)

        @block.vector
        def _(dve):
            dve.wait_ge(consts_in, 160)
            dve.wait_ge(att_in, 32)
            dve.wait_ge(pool_const, 11)
            for k in range(2):
                dve.tensor_scalar(att_diag[:, k * HEADS:(k + 1) * HEADS], head_mask[:, :], att_col[:, k:k + 1],
                                  None, ALU.mult).then_inc(dve_const, 1)
            dve.tensor_tensor(hid_bias[:, 3:4], hid_bias[:, 1:2], hid_bias[:, 2:3], ALU.mult)\
                .then_inc(dve_const, 1)
            dve.wait_ge(dve_const, 3)
            dve.tensor_tensor(hid_bias[:, 3:4], hid_bias[:, 3:4], hid_bias[:, 0:1], ALU.add)\
                .then_inc(dve_const, 1)

            dve.wait_ge(x_in, 16)

            def centre(g):
                b = slice(g * CB, (g + 1) * CB)
                dve.tensor_reduce(pstat[:, 0, b], x_pb[:, b, :], AX.X, ALU.add).then_inc(pro_chain, 1)
                dve.wait_ge(pro_chain, 4 * g + 1)
                dve.tensor_scalar(pstat[:, 1, b], pstat[:, 0, b], -1.0 / D, None, ALU.mult).then_inc(pro_chain, 1)
                dve.wait_ge(pro_chain, 4 * g + 2)
                dve.tensor_tensor(x_pb[:, b, :], x_pb[:, b, :], wide(pstat[:, 1, b], CB), ALU.add)\
                    .then_inc(pro_chain, 1)
                dve.wait_ge(pro_chain, 4 * g + 3)
                dve.tensor_tensor(squares[:, :, :], x_pb[:, b, :], x_pb[:, b, :], ALU.mult).then_inc(pro_chain, 1)
                dve.wait_ge(pro_chain, 4 * g + 4)
                dve.tensor_reduce(pstat[:, 2, b], squares[:, :, :], AX.X, ALU.add).then_inc(pro_var, 1)
                dve.wait_ge(pro_var, g + 1)

            def normalise(g):
                b = slice(g * CB, (g + 1) * CB)
                dve.wait_ge(pro_std, g + 1)
                dve.reciprocal(pstat[:, 4, b], pstat[:, 3, b]).then_inc(pro_norm, 1)
                dve.wait_ge(pro_norm, 2 * g + 1)
                dve.tensor_tensor(x_pb[:, b, :], x_pb[:, b, :], wide(pstat[:, 4, b], CB), ALU.mult)\
                    .then_inc(pro_norm, 1)

            for g in range(NC):
                centre(g)
                if g:
                    normalise(g - 1)
            normalise(NC - 1)

            def fold_chunk(s, c):
                n = s * NC + c
                dve.wait_ge(chunk_in[c % RING], s * (16 * NC // RING) + 16 * (c // RING + 1))
                lo, hi = slot(c)[:, 0:HALF], slot(c)[:, HALF:2 * HALF]
                if c == 0:
                    dve.tensor_tensor(max_lo[:, :], lo, hi, ALU.max).then_inc(hi_done, 1)
                elif c == 1:
                    dve.tensor_tensor(max_hi[:, :], lo, hi, ALU.max).then_inc(hi_done, 1)
                else:
                    dve.wait_ge(hi_done, n)
                    dve.tensor_tensor(max_lo[:, :], max_lo[:, :], lo, ALU.max).then_inc(lo_done, 1)
                    dve.tensor_tensor(max_hi[:, :], max_hi[:, :], hi, ALU.max).then_inc(hi_done, 1)

            def fold_maxima(s):
                dve.wait_ge(hi_done, s * NC + NC)
                dve.wait_ge(lo_done, s * (NC - 2) + NC - 2)
                dve.tensor_tensor(max_lo[:, :], max_lo[:, :], max_hi[:, :], ALU.max).then_inc(fold, 1)
                dve.wait_ge(fold, s * 2 + 1)
                dve.tensor_tensor(max_lo[:, 0:2 * W], max_lo[:, 0:2 * W], max_lo[:, 2 * W:4 * W], ALU.max)\
                    .then_inc(fold, 1)
                dve.wait_ge(fold, s * 2 + 2)
                dve.tensor_tensor(runmax[:, :], max_lo[:, 0:W], max_lo[:, W:2 * W], ALU.max)\
                    .then_inc(runmax_done, 1)

            def search_classes(s):
                ts = bass.ds(s * TB, TB)
                dve.wait_ge(runmax_turned, s + 1)
                dve.sem_inc(dve_past, 1)
                for k in range(TB):
                    dve.max(top_cls[:, k, :], ps_max[:, k * P:(k + 1) * P]).then_inc(cls_top, 1)
                dve.wait_ge(cls_top, s * TB + TB)
                dve.sem_inc(dve_past, 1)
                for k in range(TB):
                    dve.max_index(idx_cls[:, k, :], top_cls[:, k, :], ps_max[:, k * P:(k + 1) * P])\
                        .then_inc(cls_done, 1)
                dve.tensor_copy(first[:, ts], top_cls[:, :, 0]).then_inc(top_kept, 1)
                dve.wait_ge(cls_done, s * TB + TB)
                dve.tensor_tensor(cls_row[:, :], idx_cls[:, :, 0], row_base[:, ts], ALU.add)\
                    .then_inc(cls_row_done, 1)

            def search_candidates(s):
                ts = bass.ds(s * TB, TB)
                dve.wait_ge(cand_in, s * (16 * TB) + 16 * TB)
                dve.sem_inc(dve_past, 1)
                for k in range(TB):
                    dve.max(top_cand[:, k, :], cand[:, k, :]).then_inc(cand_top, 1)
                dve.wait_ge(cand_top, s * TB + TB)
                dve.sem_inc(dve_past, 1)
                for k in range(TB):
                    dve.max_index(idx_cand[:, k, :], top_cand[:, k, :], cand[:, k, :]).then_inc(cand_done, 1)
                dve.tensor_tensor(second[:, ts], top_cls[:, :, 1], top_cand[:, :, 1], ALU.max)\
                    .then_inc(top_kept, 1)
                dve.wait_ge(cand_done, s * TB + TB)
                dve.scalar_tensor_tensor(best[:, ts], idx_cls[:, :, 0], float(NB), idx_cand[:, :, 0],
                                         ALU.mult, ALU.add).then_inc(best_done, 1)

            def residual(s):
                x1 = x_tq[:, bass.ds(s * TB, TB), :]
                c0 = s * 6
                dve.wait_ge(acc_tq_done, s + 1)
                dve.tensor_tensor(tmp[:, :, :], ps_xb[:, :, :],
                                  acc_tq[:, :, D:D + 1].to_broadcast([P, TB, D]), ALU.mult).then_inc(chain, 1)
                dve.wait_ge(chain, c0 + 1)
                dve.tensor_tensor(tmp[:, :, :], acc_tq[:, :, 0:D], tmp[:, :, :], ALU.subtract).then_inc(chain, 1)
                dve.wait_ge(chain, c0 + 2)
                dve.tensor_tensor(x1, x1, tmp[:, :, :], ALU.add).then_inc(x1_done, 1)
                dve.wait_ge(x1_done, s + 1)
                dve.sem_inc(dve_past, 1)
                dve.tensor_reduce(stat[:, 0, :], x1, AX.X, ALU.add).then_inc(chain, 1)
                dve.wait_ge(chain, c0 + 3)
                dve.tensor_scalar(stat[:, 1, :], stat[:, 0, :], -1.0 / D, None, ALU.mult).then_inc(chain, 1)
                dve.wait_ge(chain, c0 + 4)
                dve.tensor_tensor(cen[:, :, :], x1, wide(stat[:, 1, :], TB), ALU.add).then_inc(chain, 1)
                dve.wait_ge(chain, c0 + 5)
                dve.tensor_tensor(tmp[:, :, :], cen[:, :, :], cen[:, :, :], ALU.mult).then_inc(chain, 1)
                dve.wait_ge(chain, c0 + 6)
                dve.tensor_reduce(stat[:, 2, :], tmp[:, :, :], AX.X, ALU.add).then_inc(var_done, 1)

            def scale_h1(s):
                dve.wait_ge(std_done, s + 1)
                dve.reciprocal(rstd[:, :], stat[:, 3, :]).then_inc(h1_done, 1)
                dve.wait_ge(h1_done, 2 * s + 1)
                dve.tensor_tensor(h1[:, :, :], cen[:, :, :], wide(rstd[:, :], TB), ALU.mult).then_inc(h1_done, 1)

            def score_bound(s):
                dve.wait_ge(feat_done, s + 1)
                dve.sem_inc(dve_past, 1)
                dve.tensor_reduce(score_max[:, bass.ds(s, 1)], feats_v[:, bass.ds(s * TB, TB), D:FA], AX.XY,
                                  ALU.max, apply_absolute_value=True).then_inc(score_done, 1)

            def first_strip():
                for c in range(NC):
                    fold_chunk(0, c)
                fold_maxima(0)

            def strip(s):
                dve.wait_ge(runmax_done, s)
                for c in range(NC):
                    fold_chunk(s, c)
                    if c == 3:
                        search_classes(s - 1)
                        residual(s - 1)
                    if c == 4:
                        scale_h1(s - 1)
                    if c == 6:
                        search_candidates(s - 1)
                dve.wait_ge(runmax_turned, s)
                fold_maxima(s)
                score_bound(s - 1)

            dve.wait_ge(x_tq_in, 16)
            first_strip()
            with dve.Fori(1, S) as s:
                strip(s)
            search_classes(S - 1)
            residual(S - 1)
            scale_h1(S - 1)
            search_candidates(S - 1)
            score_bound(S - 1)

            dve.wait_ge(top_kept, 2 * S)
            dve.tensor_scalar(gap[:, 1, :], first[:, :], -1.0, MASK, ALU.add, ALU.mult).then_inc(end_chain, 1)
            dve.tensor_scalar(gap[:, 2, :], second[:, :], -1.0, MASK, ALU.add, ALU.mult).then_inc(end_chain, 1)
            dve.wait_ge(end_chain, 2)
            dve.tensor_tensor(gap[:, 3, :], gap[:, 1, :], gap[:, 2, :], ALU.subtract).then_inc(end_chain, 1)
            dve.wait_ge(end_chain, 3)
            dve.tensor_reduce(good[:, 0:1], gap[:, 3, :], AX.X, ALU.min).then_inc(end_chain, 1)
            dve.wait_ge(score_done, S)
            dve.tensor_reduce(good[:, 1:2], score_max[:, :], AX.X, ALU.max).then_inc(end_chain, 1)
            dve.wait_ge(end_chain, 5)
            dve.tensor_scalar(good[:, 2:3], good[:, 0:1], LEAD, None, ALU.is_ge).then_inc(end_chain, 1)
            dve.wait_ge(end_chain, 6)
            dve.scalar_tensor_tensor(good[:, 3:4], good[:, 1:2], HALF_SCORE, good[:, 2:3], ALU.is_le, ALU.mult)\
                .then_inc(good_done, 1)
            dve.wait_ge(good_count, 1)
            dve.tensor_scalar(flag[:, :], ps_hid[0:1, 0:1], P - 0.5, None, ALU.is_lt).then_inc(flag_done, 1)

            for g in range(QG):
                ts = slice(g * OG, (g + 1) * OG)
                dve.wait_ge(got[g], 16 * OG)
                dve.tensor_tensor(gathered[:, ts, :], gathered[:, ts, :],
                                  bias_row[:, :].unsqueeze(1).to_broadcast([P, OG, D]), ALU.add).then_inc(biased, 1)
                dve.wait_ge(biased, g + 1)
                dve.scalar_tensor_tensor(gathered[:, ts, :].rearrange("q t d -> q (t d)"),
                                         gathered[:, ts, :].rearrange("q t d -> q (t d)"), 0.0,
                                         x_tq[:, ts, :].rearrange("q t d -> q (t d)"),
                                         ALU.max, ALU.add).then_inc(out_done, 1)

            dve.wait_ge(flag_done, 1)
            general = dve.value_load(flag[0:1, 0:1], min_val=0, max_val=1)
            with dve.If(general != 0):
                row, neigh, sc = ring[:, 0:N], ring[:, N:2 * N], h_t[:, :]
                for g in range(NB // 4):
                    dve.wait_ge(gen_turned, g + 1)
                    dve.tensor_copy(h_t[0:HEADS, g * W:(g + 1) * W], acc[g % 2][0:HEADS, :]).then_inc(gen_copied, 1)
                dve.wait_ge(out_done, QG)
                dve.wait_ge(stored, 16 * QG)
                dve.sem_inc(gen_head, 1)
                with dve.Fori(0, NB) as ib:
                    dve.wait_ge(gen_row_in, ib * 16 + 16)
                    dve.tensor_scalar(row, row, -1.0, MASK, ALU.add, ALU.mult).then_inc(gen_mask, 1)
                    with dve.Fori(0, HEADS) as h:
                        n = ib * HEADS + h
                        c0 = n * 7
                        dve.wait_ge(gen_neigh_in, n * 16 + 16)
                        dve.tensor_copy(gap[:, 3, 0:1], feats[:, bass.ds(ib * FA + D + h, 1)]).then_inc(gen_chain, 1)
                        dve.wait_ge(gen_chain, c0 + 1)
                        dve.tensor_scalar(sc, neigh, gap[:, 3, 0:1], None, ALU.add).then_inc(gen_chain, 1)
                        dve.wait_ge(gen_chain, c0 + 2)
                        dve.scalar_tensor_tensor(sc, sc, SLOPE, sc, ALU.mult, ALU.max).then_inc(gen_chain, 1)
                        dve.wait_ge(gen_chain, c0 + 3)
                        dve.wait_ge(gen_mask, ib * 2 + 1)
                        dve.tensor_tensor(sc, sc, row, ALU.add).then_inc(gen_chain, 1)
                        dve.wait_ge(gen_chain, c0 + 4)
                        dve.tensor_reduce(gap[:, 0, 0:1], sc, AX.X, ALU.max).then_inc(gen_chain, 1)
                        dve.wait_ge(gen_chain, c0 + 5)
                        dve.tensor_scalar(gap[:, 1, 0:1], gap[:, 0, 0:1], -1.0, None, ALU.mult).then_inc(gen_max, 1)
                        for g in range(NB // 4):
                            dve.wait_ge(gen_p_turned, n * (NB // 4) + g + 1)
                            dve.tensor_copy(max_lo[:, (g % 2) * W:(g % 2 + 1) * W], acc[g % 2][:, :])\
                                .then_inc(gen_p_copied, 1)
                        dve.wait_ge(gen_exp, n + 1)
                        dve.reciprocal(gap[:, 3, 1:2], gap[:, 2, 0:1]).then_inc(gen_chain, 1)
                        dve.wait_ge(gen_chain, c0 + 6)
                        dve.wait_ge(gen_sum, n + 1)
                        dve.tensor_scalar(cen[:, 0:1, :].rearrange("q a d -> q (a d)")[:, bass.ds(h * HD, HD)],
                                          ps_hid[:, 0:HD], gap[:, 3, 1:2], None, ALU.mult).then_inc(gen_chain, 1)
                        dve.wait_ge(gen_chain, c0 + 7)
                        dve.sem_inc(gen_head, 1)
                    dve.tensor_tensor(h1[:, 0, :], cen[:, 0, :], bias_row[:, :], ALU.add).then_inc(gen_mask, 1)
                    dve.wait_ge(gen_mask, ib * 2 + 2)
                    dve.scalar_tensor_tensor(tmp[:, 0, :], h1[:, 0, :], 0.0,
                                             x_tq[:, bass.ds(ib, 1), :].rearrange("q a d -> q (a d)"),
                                             ALU.max, ALU.add).then_inc(gen_out, 1)

        @block.tensor
        def _(pe):
            pe.wait_ge(pool_const, 11)
            pe.wait_ge(dve_const, 2)
            pe.matmul(ps_feat[0:D, 0, 0:2 * HEADS], w_gat_t_sb[:, :], att_diag[:, :], start=True, stop=True)\
                .then_inc(w_ext_ready, 1)

            def first_group(g):
                pe.wait_ge(pro_norm, 2 * g + 2)
                if g:
                    pe.wait_ge(pro_h, 2 * g)
                for k in range(CB):
                    dst = (psh if k < 4 else psr_h)[:, k % 4, :]
                    last = pe.transpose(dst, x_pb[:, g * CB + k, :], ident[:, :])
                last.then_inc(pro_turned, 1)
                pe.wait_ge(pro_h, 2 * g + 2)
                if g:
                    pe.wait_ge(xb_done, g)
                for k in range(CB):
                    last = pe.matmul(ps_hid[:, k * D:(k + 1) * D], h_by_block[:, g * CB + k, :], b_t_sb[:, :],
                                     start=True, stop=True)
                last.then_inc(pro_xb, 1)

            def chunk(s, c, parity):
                pe.wait_ge(chunk_in[c % RING], s * (16 * NC // RING) + 16 * (c // RING + 1))
                for b in range(CB):
                    last = pe.matmul(acc[parity][0:D + 1, :], xb_ones[:, c * CB + b, :],
                                     slot(c)[:, b * W:(b + 1) * W], start=(c == 0 and b == 0), stop=False)
                last.then_inc(pe_chunk, 1)

            def mlp_hidden(s):
                pe.wait_ge(strip_h_done, s + 1)
                pe.matmul(ps_hid[:, :], w1_sb[:, :], h_strip[:, :], start=True, stop=True).then_inc(hid_ready, 1)

            def mlp_out(s, parity):
                pe.wait_ge(hid_done, s + 1)
                pe.matmul(acc[parity][0:D + 1, :], w2_sb[:, :], hidden[:, :], start=False, stop=True)\
                    .then_inc(acc_ready, 1)

            def turn_sums(s):
                pe.wait_ge(acc_copied, s + 1)
                for k in range(TB):
                    pe.transpose(ps_acc[:, k, :], acc_sb[:, k * P:(k + 1) * P], ident[0:D + 1, 0:D + 1])
                for k in range(TB):
                    last = pe.matmul(ps_xb[:, k, :], h_strip[:, k * P:(k + 1) * P], b_t_sb[:, :],
                                     start=True, stop=True)
                last.then_inc(acc_turned, 1)

            def turn_maxima(s):
                pe.wait_ge(runmax_done, s + 1)
                for k in range(TB):
                    last = pe.transpose(ps_max[:, k * P:(k + 1) * P], runmax[:, k * P:(k + 1) * P], ident[:, :])
                last.then_inc(runmax_turned, 1)

            def turn_h1(s):
                pe.wait_ge(h1_done, 2 * s + 2)
                pe.sem_inc(pe_past, 1)
                for k in range(TB):
                    last = pe.transpose(psh[:, k, :], h1[:, k, :], ident[:, :])
                last.then_inc(h1_turned, 1)

            def features(s):
                pe.wait_ge(h1_t_done, s + 1)
                for k in range(TB):
                    last = pe.matmul(ps_feat[:, k, :], h1_t[:, k * P:(k + 1) * P], w_ext[:, :],
                                     start=True, stop=True)
                last.then_inc(feat_ready, 1)

            def strip(s, parity):
                for c in range(NC):
                    chunk(s, c, parity)
                    if c == 0:
                        turn_maxima(s - 1)
                        turn_sums(s - 1)
                    if c == 3:
                        turn_h1(s - 1)
                    if c == 4:
                        features(s - 1)
                    if c == 5:
                        mlp_hidden(s)
                mlp_out(s, parity)

            first_group(0)
            for c in range(NC):
                if c + 1 < NC:
                    first_group(c + 1)
                pe.wait_ge(xb_done, c + 1)
                chunk(0, c, 0)
            pe.wait_ge(w_ext_done, 1)
            mlp_hidden(0)
            mlp_out(0, 0)
            with pe.Fori(0, S // 2 - 1) as r:
                strip(2 * r + 1, 1)
                strip(2 * r + 2, 0)
            strip(S - 1, 1)
            turn_maxima(S - 1)
            turn_sums(S - 1)
            turn_h1(S - 1)
            features(S - 1)
            pe.wait_ge(good_done, 1)
            pe.matmul(ps_hid[0:1, 0:1], good[:, 3:4], ones[:, :], start=True, stop=True).then_inc(good_count, 1)

            pe.wait_ge(flag_done, 1)
            general = pe.value_load(flag[0:1, 0:1], min_val=0, max_val=1)
            with pe.If(general != 0):
                for g in range(NB // 4):
                    if g >= 2:
                        pe.wait_ge(gen_copied, g - 1)
                    for k in range(4):
                        last = pe.transpose(acc[g % 2][0:HEADS, k * P:(k + 1) * P],
                                            feats_v[:, g * 4 + k, D + HEADS:FA], ident[:, :])
                    last.then_inc(gen_turned, 1)
                with pe.Fori(0, NB) as ib:
                    with pe.Fori(0, HEADS) as h:
                        n = ib * HEADS + h

                        def turn(g):
                            if g >= 2:
                                pe.wait_ge(gen_p_copied, n * (NB // 4) + g - 1)
                            for k in range(4):
                                j = g * 4 + k
                                last = pe.transpose(acc[g % 2][:, k * P:(k + 1) * P],
                                                    h_t[:, j * P:(j + 1) * P], ident[:, :])
                            last.then_inc(gen_p_turned, 1)

                        pe.wait_ge(gen_exp, n + 1)
                        turn(0)
                        for g in range(NB // 4):
                            if g + 1 < NB // 4:
                                turn(g + 1)
                            pe.wait_ge(gen_p_copied, n * (NB // 4) + g + 1)
                            for k in range(4):
                                j = g * 4 + k
                                at = (g % 2) * W + k * P
                                last = pe.matmul(ps_hid[:, 0:HD], max_lo[:, at:at + P],
                                                 feats[:, bass.ds(h * HD + j * FA, HD)],
                                                 start=(j == 0), stop=(j == NB - 1))
                        last.then_inc(gen_sum, 1)


def kernel(x, adj, L0_gnn_t, L0_gnn_B, L0_gnn_W1, L0_gnn_b1, L0_gnn_W2, L0_gnn_b2,
           L1_gnn_W, L1_gnn_att_self, L1_gnn_att_neigh, L1_gnn_bias):
    import numpy as np
    import concourse.bacc as bacc
    from concourse.bass_utils import run_bass_kernel_spmd

    adj = np.asarray(adj)
    w1 = np.asarray(L0_gnn_W1)
    w_gat = np.asarray(L1_gnn_W)
    tiles = adj.reshape(S, W, P, NC, CB).transpose(0, 3, 2, 4, 1)
    arrays = {
        "x": x,
        "adj": adj,
        "adj_t": tiles.reshape(S * NC, P, CB * W),
        "w1": w1[0:D],
        "w1_t": w1[D:D + 1].reshape(HID, 1),
        "b1": np.asarray(L0_gnn_b1).reshape(HID, 1),
        "t_in": np.asarray(L0_gnn_t).reshape(1, 1),
        "w2": L0_gnn_W2,
        "b2": np.asarray(L0_gnn_b2).reshape(D, 1),
        "b_t": np.asarray(L0_gnn_B).T,
        "w_gat": w_gat,
        "w_gat_t": w_gat.T,
        "att_self": np.asarray(L1_gnn_att_self).reshape(D, 1),
        "att_neigh": np.asarray(L1_gnn_att_neigh).reshape(D, 1),
        "bias": np.asarray(L1_gnn_bias).reshape(1, D),
    }
    nc = bacc.Bacc("TRN2", target_bir_lowering=False, num_devices=1)
    arrays = {f"in_{n}": np.ascontiguousarray(a) for n, a in arrays.items()}
    ins = [nc.dram_tensor(n, a.shape, mybir.dt.from_np(a.dtype), kind="ExternalInput").ap() for n, a in arrays.items()]
    out = nc.dram_tensor("out", (N, D), F32, kind="ExternalOutput").ap()
    build(nc, *ins, out)
    r = run_bass_kernel_spmd(nc, [arrays], core_ids=[0])
    return r.results[0]["out"]
```

```python
from contextlib import ExitStack

import concourse.bass as bass
from concourse import mybir

F32 = mybir.dt.float32
I32 = mybir.dt.int32
U32 = mybir.dt.uint32
ALU = mybir.AluOpType
ACT = mybir.ActivationFunctionType
AX = mybir.AxisListType

P = 128
N = 8192
D = 64
HID = 128
HEADS, HD = 8, 8
NB = N // P
W = 512
S = N // W
TB = W // P
CB = 8
NC = NB // CB
RING = 4
HALF = CB * W // 2
QUAD = 32
FA = D + 2 * HEADS
EPS = 1e-5
SLOPE = 0.2
MASK = 1e10
LEAD = 505.0
HALF_SCORE = 50.0
OG = 8
QG = NB // OG


def build(nc, x, adj, adj_t, w1, w1_t, b1, t_in, w2, b2, b_t, w_gat, w_gat_t, att_self, att_neigh, bias, out):
    with ExitStack() as ctx:
        def sb(name, shape, dt=F32):
            return ctx.enter_context(nc.sbuf_tensor(name, shape, dt))

        def pb(name, shape, dt=F32):
            return ctx.enter_context(nc.psum_tensor(name, shape, dt))

        def sem(name):
            return ctx.enter_context(nc.semaphore(name))

        feats_dram = nc.dram_tensor("feats_dram", (N, D), F32, kind="Internal").ap()
        neigh_dram = nc.dram_tensor("neigh_dram", (HEADS, N), F32, kind="Internal").ap()

        ring = sb("ring", [P, RING * CB * W])
        gathered = sb("gathered", [P, NB, D])
        ones_cols = sb("ones_cols", [P, QUAD])
        h_t = sb("h_t", [P, N])
        x_pb = sb("x_pb", [P, NB, D])
        x_tq = sb("x_tq", [P, NB, D])
        feats = sb("feats", [P, NB * FA])
        max_lo = sb("max_lo", [P, HALF])
        max_hi = sb("max_hi", [P, HALF])
        cand = sb("cand", [P, TB, NB])
        hidden = sb("hidden", [HID, W])
        acc_sb = sb("acc_sb", [P, W])
        row_sb = sb("row_sb", [P, W])
        acc_tq = sb("acc_tq", [P, TB, D + 1])
        tmp = sb("tmp", [P, TB, D])
        cen = sb("cen", [P, TB, D])
        h1 = sb("h1", [P, TB, D])
        h1_t = sb("h1_t", [D, W])
        h_strip = sb("h_strip", [D, W])
        stat = sb("stat", [P, 4, TB])
        rstd = sb("rstd", [P, TB])
        squares = [acc_sb, row_sb]
        pstat = sb("pstat", [P, 5, NB])
        ident = sb("ident", [P, P])
        b_t_twice = sb("b_t_twice", [P, D])
        w1_sb = sb("w1_sb", [D, HID])
        w2_sb = sb("w2_sb", [HID, D])
        hid_bias = sb("hid_bias", [HID, 4])
        b2_row = sb("b2_row", [P, D])
        fold_rows = sb("fold_rows", [P, 1])
        w_ext = sb("w_ext", [D, FA])
        w_gat_t_sb = sb("w_gat_t_sb", [D, D])
        att_diag = sb("att_diag", [D, 2 * HEADS])
        att_col = sb("att_col", [D, 2])
        head_mask = sb("head_mask", [D, HEADS])
        bias_row = sb("bias_row", [P, D])
        eps = sb("eps", [P, 1])
        ones = sb("ones", [P, 1])
        row_base = sb("row_base", [P, NB], I32)
        runmax = sb("runmax", [P, W])
        top_cls = sb("top_cls", [P, TB, 8])
        idx_cls = sb("idx_cls", [P, TB, 8], U32)
        top_cand = sb("top_cand", [P, TB, 8])
        idx_cand = sb("idx_cand", [P, TB, 8], U32)
        cls_row = sb("cls_row", [P, TB], U32)
        first = sb("first", [P, NB])
        second = sb("second", [P, NB])
        best = sb("best", [P, NB], U32)
        score_max = sb("score_max", [P, S])
        gap = sb("gap", [P, 4, NB])
        good = sb("good", [P, 4])
        flag = sb("flag", [1, 1], I32)

        acc = [pb(f"acc{i}", [P, W]) for i in range(2)]
        row_sums = pb("row_sums", [P, W])
        ps_hid = pb("ps_hid", [P, W])
        ps_acc_bank = pb("ps_acc_bank", [P, W])
        ps_acc = ps_acc_bank[:, 0:TB * (D + 1)].rearrange("q (t f) -> q t f", f=D + 1)
        ps_xb = pb("ps_xb", [P, TB, D])
        ps_turn = pb("ps_turn", [P, W])
        ps_feat = pb("ps_feat", [P, TB, FA])

        consts_in = sem("consts_in")
        att_in = sem("att_in")
        x_b2_done = sem("x_b2_done")
        x_in = [sem(f"x_in{k}") for k in range(2)]
        x_tq_in = sem("x_tq_in")
        w_in = sem("w_in")
        pool_const = sem("pool_const")
        dve_const = sem("dve_const")
        w_ext_ready = sem("w_ext_ready")
        w_ext_done = sem("w_ext_done")
        pro_chain = sem("pro_chain")
        pro_centred = sem("pro_centred")
        pro_squared = sem("pro_squared")
        pro_var = sem("pro_var")
        pro_recip = sem("pro_recip")
        pro_std = sem("pro_std")
        pro_norm = sem("pro_norm")
        pro_turned = sem("pro_turned")
        pro_h = sem("pro_h")
        pro_xb = sem("pro_xb")
        xb_done = sem("xb_done")
        chunk_in = [sem(f"chunk_in{r}") for r in range(RING)]
        pe_chunk = sem("pe_chunk")
        lo_done = sem("lo_done")
        hi_done = sem("hi_done")
        fold = sem("fold")
        hid_ready = sem("hid_ready")
        hid_done = sem("hid_done")
        strip_h_done = sem("strip_h_done")
        acc_copied = sem("acc_copied")
        rows_copied = sem("rows_copied")
        acc_turned = sem("acc_turned")
        acc_tq_done = sem("acc_tq_done")
        chain = sem("chain")
        x1_done = sem("x1_done")
        var_done = sem("var_done")
        std_done = sem("std_done")
        h1_done = sem("h1_done")
        h1_turned = sem("h1_turned")
        h1_t_done = sem("h1_t_done")
        feat_ready = sem("feat_ready")
        feat_done = sem("feat_done")
        feat_stored = sem("feat_stored")
        score_done = sem("score_done")
        runmax_done = sem("runmax_done")
        runmax_turned = sem("runmax_turned")
        cls_top = sem("cls_top")
        cls_done = sem("cls_done")
        cls_row_done = sem("cls_row_done")
        cand_in = sem("cand_in")
        cand_top = sem("cand_top")
        cand_done = sem("cand_done")
        top_kept = sem("top_kept")
        best_done = sem("best_done")
        got = [sem(f"got{g}") for g in range(QG)]
        end_chain = sem("end_chain")
        good_done = sem("good_done")
        good_count = sem("good_count")
        flag_done = sem("flag_done")
        biased = sem("biased")
        rectified = sem("rectified")
        out_done = sem("out_done")
        stored = sem("stored")
        sp_past = sem("sp_past")
        pool_past = sem("pool_past")
        dve_past = sem("dve_past")
        pe_past = sem("pe_past")
        gen_turned = sem("gen_turned")
        gen_copied = sem("gen_copied")
        gen_neigh_stored = sem("gen_neigh_stored")
        gen_row_in = sem("gen_row_in")
        gen_neigh_in = sem("gen_neigh_in")
        gen_chain = sem("gen_chain")
        gen_mask = sem("gen_mask")
        gen_max = sem("gen_max")
        gen_exp = sem("gen_exp")
        gen_p_turned = sem("gen_p_turned")
        gen_p_copied = sem("gen_p_copied")
        gen_sum = sem("gen_sum")
        gen_head = sem("gen_head")
        gen_out = sem("gen_out")
        gen_stored = sem("gen_stored")

        x_by_p = x.rearrange("(p b) d -> p b d", b=NB)
        x_by_q = x.rearrange("(t q) d -> q t d", q=P)
        out_by_q = out.rearrange("(t q) d -> q t d", q=P)
        feats_by_q = feats_dram.rearrange("(t q) d -> q t d", q=P)
        classes = adj.rearrange("i (p b) -> (i p) b", b=NB)
        h_by_block = h_t[0:D, :].rearrange("d (p b) -> d b p", b=NB)
        feats_v = feats[:, :].rearrange("q (t f) -> q t f", f=FA)
        pro_banks = [ps_turn[0:D, :].rearrange("d (k q) -> d k q", q=P),
                     ps_acc_bank[0:D, :].rearrange("d (k q) -> d k q", q=P)]

        def slot(n):
            return ring[:, (n % RING) * CB * W:(n % RING + 1) * CB * W]

        def wide(a, k, n=D):
            return a.unsqueeze(2).to_broadcast([P, k, n])

        block = ctx.enter_context(nc.Block())

        @block.sync
        def _(sp):
            for k, (b0, b1_) in enumerate(((0, 2 * CB), (2 * CB, NB))):
                sp.dma_start(x_pb[:, b0:b1_, :], x_by_p[:, b0:b1_, :]).then_inc(x_in[k], 16)
            for n in range(RING):
                sp.dma_start(slot(n), adj_t[n]).then_inc(chunk_in[n % RING], 16)
            sp.dma_start(x_tq[:, :, :], x_by_q).then_inc(x_tq_in, 16)

            def load(s, c):
                sp.wait_ge(pe_chunk, s * NC + (c - RING + 1))
                sp.wait_ge(hi_done, s * NC + (c - RING + 1))
                sp.sem_inc(sp_past, 1)
                src = adj_t[bass.ds(s * NC + c, 1)].rearrange("a p f -> (a p) f")
                sp.dma_start(slot(c), src).then_inc(chunk_in[c % RING], 16)

            def store_feats(s):
                sp.wait_ge(feat_done, s + 1)
                sp.sem_inc(sp_past, 1)
                sp.dma_start(feats_by_q[:, bass.ds(s * TB, TB), :],
                             feats_v[:, bass.ds(s * TB, TB), 0:D]).then_inc(feat_stored, 16)

            for c in range(RING, NC):
                load(0, c)
            with sp.Fori(1, S) as s:
                for c in range(NC):
                    load(s, c)
                store_feats(s - 1)
            store_feats(S - 1)
            for g in range(QG):
                sp.wait_ge(out_done, g + 1)
                ts = slice(g * OG, (g + 1) * OG)
                sp.dma_start(out_by_q[:, ts, :], gathered[:, ts, :]).then_inc(stored, 16)
            sp.wait_ge(stored, 16 * QG)

            sp.wait_ge(flag_done, 1)
            general = sp.value_load(flag[0:1, 0:1], min_val=0, max_val=1)
            with sp.If(general != 0):
                sp.wait_ge(gen_copied, NB // 4)
                sp.dma_start(neigh_dram, h_t[0:HEADS, :]).then_inc(gen_neigh_stored, 16)
                sp.wait_ge(gen_neigh_stored, 16)
                with sp.Fori(0, NB) as ib:
                    sp.wait_ge(gen_head, ib * HEADS + 1)
                    sp.sem_inc(sp_past, 1)
                    rows = adj.rearrange("(t q) j -> t q j", q=P)[bass.ds(ib, 1)]
                    sp.dma_start(ring[:, 0:N], rows.rearrange("a q j -> (a q) j")).then_inc(gen_row_in, 16)
                    with sp.Fori(0, HEADS) as h:
                        sp.wait_ge(gen_head, ib * HEADS + h + 1)
                        sp.sem_inc(sp_past, 1)
                        sp.dma_start(ring[:, N:2 * N], neigh_dram[bass.ds(h, 1), :].to_broadcast([P, N]))\
                            .then_inc(gen_neigh_in, 16)
                    sp.wait_ge(gen_out, ib + 1)
                    sp.sem_inc(sp_past, 1)
                    dst = out.rearrange("(t q) d -> t q d", q=P)[bass.ds(ib, 1)]
                    sp.dma_start(dst.rearrange("a q d -> (a q) d"), tmp[:, 0, :]).then_inc(gen_stored, 16)
                    sp.wait_ge(gen_stored, ib * 16 + 16)
                    sp.sem_inc(sp_past, 1)

        @block.gpsimd
        def _(pool):
            for n, (dst, value) in enumerate(((ones[:, :], 1.0), (eps[:, :], EPS), (ones_cols[:, :], 1.0),
                                              (head_mask[:, :], 1.0), (ident[:, :], 0.0))):
                pool.memset(dst, value).then_inc(pool_const, 1)
                pool.wait_ge(pool_const, n + 1)
            pool.affine_select(out=ident[:, :], in_=ident[:, :], compare_op=ALU.not_equal, fill=1.0,
                               base=0, pattern=[[-1, P]], channel_multiplier=1).then_inc(pool_const, 1)
            pool.wait_ge(pool_const, 6)
            pool.affine_select(out=head_mask[:, :], in_=head_mask[:, :], compare_op=ALU.is_ge, fill=0.0,
                               base=0, pattern=[[-HD, HEADS]], channel_multiplier=1).then_inc(pool_const, 1)
            pool.wait_ge(pool_const, 7)
            pool.affine_select(out=head_mask[:, :], in_=head_mask[:, :], compare_op=ALU.is_ge, fill=0.0,
                               base=HD - 1, pattern=[[HD, HEADS]], channel_multiplier=-1)\
                .then_inc(pool_const, 1)
            pool.wait_ge(pool_const, 8)
            pool.iota(row_base[:, :], pattern=[[P * P, NB]], base=0, channel_multiplier=P)\
                .then_inc(pool_const, 1)

            pool.wait_ge(consts_in, 176)
            pool.wait_ge(x_tq_in, 16)
            pool.tensor_tensor(x_tq[:, :, :], x_tq[:, :, :], b2_row[:, :].unsqueeze(1).to_broadcast([P, NB, D]),
                               ALU.add).then_inc(x_b2_done, 1)

            with pool.Fori(0, S) as s:
                pool.wait_ge(cls_row_done, s + 1)
                pool.sem_inc(pool_past, 1)
                for k in range(TB):
                    pool.indirect_dma_start(
                        out=cand[:, k, :], out_offset=None, in_=classes,
                        in_offset=bass.IndirectOffsetOnAxis(ap=cls_row[:, k:k + 1], axis=0),
                    ).then_inc(cand_in, 16)
            pool.wait_ge(feat_stored, 16 * S)
            pool.wait_ge(best_done, S - 1)
            for t in range(NB):
                if t == NB - TB:
                    pool.wait_ge(best_done, S)
                pool.indirect_dma_start(
                    out=gathered[:, t, :], out_offset=None, in_=feats_dram,
                    in_offset=bass.IndirectOffsetOnAxis(ap=best[:, t:t + 1], axis=0),
                ).then_inc(got[t // OG], 16)

        @block.scalar
        def _(act):
            act.wait_ge(pool_const, 9)

            def load_weights():
                for dst, src in ((w_gat_t_sb[:, :], w_gat_t), (w1_sb[:, :], w1), (w2_sb[:, :], w2),
                                 (hid_bias[:, 0:1], b1), (hid_bias[:, 1:2], w1_t),
                                 (hid_bias[:, 2:3], t_in.to_broadcast([HID, 1])),
                                 (b_t_twice[0:D, :], b_t), (b_t_twice[D:P, :], b_t), (b2_row[:, :], b2.to_broadcast([P, D])),
                                 (w_ext[:, 0:D], w_gat), (bias_row[:, :], bias.to_broadcast([P, D]))):
                    act.dma_start(dst, src).then_inc(consts_in, 16)
                act.dma_start(att_col[:, 0:1], att_self).then_inc(att_in, 16)
                act.dma_start(att_col[:, 1:2], att_neigh).then_inc(att_in, 16)

            def square(g):
                act.wait_ge(pro_centred, g + 1)
                if g >= 2:
                    act.wait_ge(pro_var, g - 1)
                act.activation(squares[g % 2][:, :], x_pb[:, g * CB:(g + 1) * CB, :].rearrange("p b d -> p (b d)"),
                               ACT.Square).then_inc(pro_squared, 1)

            def deviation(g):
                act.wait_ge(pro_var, g + 1)
                act.activation(pstat[:, 3, g * CB:(g + 1) * CB], pstat[:, 2, g * CB:(g + 1) * CB], ACT.Sqrt,
                               bias=eps[:, :], scale=1.0 / D).then_inc(pro_std, 1)

            def place(g):
                act.wait_ge(pro_turned, g + 1)
                for half, src in enumerate(pro_banks):
                    b = g * CB + half * 4
                    act.copy(h_by_block[:, b:b + 4, :], src).then_inc(pro_h, 1)

            for g in range(NC + 2):
                if g < NC:
                    square(g)
                if g == 0:
                    load_weights()
                if 1 <= g <= NC:
                    deviation(g - 1)
                if g >= 2:
                    place(g - 2)
            act.wait_ge(w_ext_ready, 1)
            act.copy(w_ext[:, D:FA], ps_feat[0:D, 0, 0:2 * HEADS]).then_inc(w_ext_done, 1)

            def tanh(s):
                act.wait_ge(hid_ready, s + 1)
                act.activation(hidden[:, :], ps_hid[:, :], ACT.Tanh, bias=hid_bias[:, 3:4])\
                    .then_inc(hid_done, 1)

            def strip_h(s):
                act.copy(h_strip[:, :], h_t[0:D, bass.ds(s * W, W)]).then_inc(strip_h_done, 1)

            def finish_strip(s, parity, last=False):
                act.wait_ge(pe_chunk, s * NC + NC)
                act.copy(acc_sb[:, :], acc[parity][:, :]).then_inc(acc_copied, 1)
                act.copy(row_sb[:, :], row_sums[:, :]).then_inc(rows_copied, 1)
                act.wait_ge(acc_turned, s + 1)
                act.copy(acc_tq[:, :, :], ps_acc[:, :, :]).then_inc(acc_tq_done, 1)
                if not last:
                    strip_h(s + 1)
                act.wait_ge(var_done, s + 1)
                act.activation(stat[:, 3, :], stat[:, 2, :], ACT.Sqrt, bias=eps[:, :], scale=1.0 / D)\
                    .then_inc(std_done, 1)
                act.wait_ge(h1_turned, s + 1)
                act.activation(h1_t[:, :], (ps_hid if last else ps_turn)[0:D, :], ACT.Relu).then_inc(h1_t_done, 1)
                act.wait_ge(feat_ready, s + 1)
                act.copy(feats[:, bass.ds(s * (TB * FA), TB * FA)],
                         ps_feat[:, :, :].rearrange("q t f -> q (t f)")).then_inc(feat_done, 1)

            act.wait_ge(pro_h, 2 * NC)
            strip_h(0)
            act.wait_ge(dve_const, 5)
            tanh(0)
            with act.Fori(0, S // 2 - 1) as r:
                for k in range(2):
                    finish_strip(2 * r + k, k)
                    tanh(2 * r + k + 1)
            finish_strip(S - 2, 0)
            tanh(S - 1)
            finish_strip(S - 1, 1, last=True)

            act.wait_ge(flag_done, 1)
            general = act.value_load(flag[0:1, 0:1], min_val=0, max_val=1)
            with act.If(general != 0):
                with act.Fori(0, NB * HEADS) as n:
                    act.wait_ge(gen_max, n + 1)
                    act.activation(h_t[:, :], h_t[:, :], ACT.Exp, bias=gap[:, 1, 0:1], accum_out=gap[:, 2, 0:1])\
                        .then_inc(gen_exp, 1)

        @block.vector
        def _(dve):
            def constants():
                dve.wait_ge(consts_in, 176)
                dve.wait_ge(att_in, 32)
                dve.wait_ge(pool_const, 9)
                for k in range(2):
                    dve.tensor_scalar(att_diag[:, k * HEADS:(k + 1) * HEADS], head_mask[:, :], att_col[:, k:k + 1],
                                      None, ALU.mult).then_inc(dve_const, 1)
                dve.tensor_tensor(hid_bias[:, 3:4], hid_bias[:, 1:2], hid_bias[:, 2:3], ALU.mult)\
                    .then_inc(dve_const, 1)
                dve.wait_ge(dve_const, 3)
                dve.tensor_tensor(hid_bias[:, 3:4], hid_bias[:, 3:4], hid_bias[:, 0:1], ALU.add)\
                    .then_inc(dve_const, 1)
                dve.tensor_reduce(fold_rows[:, :], ident[:, :].rearrange("p (a b) -> p b a", b=QUAD)[:, 0, :], AX.X, ALU.add)\
                    .then_inc(dve_const, 1)

            def centre(g):
                b = slice(g * CB, (g + 1) * CB)
                dve.wait_ge(x_in[g >= 2], 16)
                dve.tensor_reduce(pstat[:, 0, b], x_pb[:, b, :], AX.X, ALU.add).then_inc(pro_chain, 1)
                dve.wait_ge(pro_chain, 2 * g + 1)
                dve.tensor_scalar(pstat[:, 1, b], pstat[:, 0, b], -1.0 / D, None, ALU.mult).then_inc(pro_chain, 1)
                dve.wait_ge(pro_chain, 2 * g + 2)
                dve.tensor_tensor(x_pb[:, b, :], x_pb[:, b, :], wide(pstat[:, 1, b], CB), ALU.add)\
                    .then_inc(pro_centred, 1)

            def variance(g):
                b = slice(g * CB, (g + 1) * CB)
                dve.wait_ge(pro_squared, g + 1)
                dve.tensor_reduce(pstat[:, 2, b], squares[g % 2][:, :].rearrange("p (b d) -> p b d", d=D),
                                  AX.X, ALU.add).then_inc(pro_var, 1)

            def normalise(g):
                b = slice(g * CB, (g + 1) * CB)
                dve.wait_ge(pro_std, g + 1)
                dve.reciprocal(pstat[:, 4, b], pstat[:, 3, b]).then_inc(pro_recip, 1)
                dve.wait_ge(pro_recip, g + 1)
                dve.scalar_tensor_tensor(x_pb[:, b, :], x_pb[:, b, :], 0.0, wide(pstat[:, 4, b], CB),
                                         ALU.max, ALU.mult).then_inc(pro_norm, 1)

            def fold_chunk(s, c):
                n = s * NC + c
                dve.wait_ge(chunk_in[c % RING], s * (16 * NC // RING) + 16 * (c // RING + 1))
                lo, hi = slot(c)[:, 0:HALF], slot(c)[:, HALF:2 * HALF]
                if c == 0:
                    dve.tensor_tensor(max_lo[:, :], lo, hi, ALU.max).then_inc(hi_done, 1)
                elif c == 1:
                    dve.tensor_tensor(max_hi[:, :], lo, hi, ALU.max).then_inc(hi_done, 1)
                else:
                    dve.wait_ge(hi_done, n)
                    dve.tensor_tensor(max_lo[:, :], max_lo[:, :], lo, ALU.max).then_inc(lo_done, 1)
                    dve.tensor_tensor(max_hi[:, :], max_hi[:, :], hi, ALU.max).then_inc(hi_done, 1)

            def fold_maxima(s):
                dve.wait_ge(hi_done, s * NC + NC)
                dve.wait_ge(lo_done, s * (NC - 2) + NC - 2)
                dve.tensor_tensor(max_lo[:, :], max_lo[:, :], max_hi[:, :], ALU.max).then_inc(fold, 1)
                dve.wait_ge(fold, s * 2 + 1)
                dve.tensor_tensor(max_lo[:, 0:2 * W], max_lo[:, 0:2 * W], max_lo[:, 2 * W:4 * W], ALU.max)\
                    .then_inc(fold, 1)
                dve.wait_ge(fold, s * 2 + 2)
                dve.tensor_tensor(runmax[:, :], max_lo[:, 0:W], max_lo[:, W:2 * W], ALU.max)\
                    .then_inc(runmax_done, 1)

            def search_classes(s):
                ts = bass.ds(s * TB, TB)
                dve.wait_ge(runmax_turned, s + 1)
                dve.sem_inc(dve_past, 1)
                for k in range(TB):
                    dve.max(top_cls[:, k, :], ps_turn[:, k * P:(k + 1) * P]).then_inc(cls_top, 1)
                dve.wait_ge(cls_top, s * TB + TB)
                dve.sem_inc(dve_past, 1)
                for k in range(TB):
                    dve.max_index(idx_cls[:, k, :], top_cls[:, k, :], ps_turn[:, k * P:(k + 1) * P])\
                        .then_inc(cls_done, 1)
                dve.tensor_copy(first[:, ts], top_cls[:, :, 0]).then_inc(top_kept, 1)
                dve.wait_ge(cls_done, s * TB + TB)
                dve.tensor_tensor(cls_row[:, :], idx_cls[:, :, 0], row_base[:, ts], ALU.add)\
                    .then_inc(cls_row_done, 1)

            def search_candidates(s):
                ts = bass.ds(s * TB, TB)
                dve.wait_ge(cand_in, s * (16 * TB) + 16 * TB)
                dve.sem_inc(dve_past, 1)
                for k in range(TB):
                    dve.max(top_cand[:, k, :], cand[:, k, :]).then_inc(cand_top, 1)
                dve.wait_ge(cand_top, s * TB + TB)
                dve.sem_inc(dve_past, 1)
                for k in range(TB):
                    dve.max_index(idx_cand[:, k, :], top_cand[:, k, :], cand[:, k, :]).then_inc(cand_done, 1)
                dve.tensor_tensor(second[:, ts], top_cls[:, :, 1], top_cand[:, :, 1], ALU.max)\
                    .then_inc(top_kept, 1)
                dve.wait_ge(cand_done, s * TB + TB)
                dve.scalar_tensor_tensor(best[:, ts], idx_cls[:, :, 0], float(NB), idx_cand[:, :, 0],
                                         ALU.mult, ALU.add).then_inc(best_done, 1)

            def residual(s):
                x1 = x_tq[:, bass.ds(s * TB, TB), :]
                c0 = s * 6
                dve.wait_ge(acc_tq_done, s + 1)
                dve.tensor_tensor(tmp[:, :, :], ps_xb[:, :, :],
                                  acc_tq[:, :, D:D + 1].to_broadcast([P, TB, D]), ALU.mult).then_inc(chain, 1)
                dve.wait_ge(chain, c0 + 1)
                dve.tensor_tensor(tmp[:, :, :], acc_tq[:, :, 0:D], tmp[:, :, :], ALU.subtract).then_inc(chain, 1)
                dve.wait_ge(chain, c0 + 2)
                dve.tensor_tensor(x1, x1, tmp[:, :, :], ALU.add).then_inc(x1_done, 1)
                dve.wait_ge(x1_done, s + 1)
                dve.sem_inc(dve_past, 1)
                dve.tensor_reduce(stat[:, 0, :], x1, AX.X, ALU.add).then_inc(chain, 1)
                dve.wait_ge(chain, c0 + 3)
                dve.tensor_scalar(stat[:, 1, :], stat[:, 0, :], -1.0 / D, None, ALU.mult).then_inc(chain, 1)
                dve.wait_ge(chain, c0 + 4)
                dve.tensor_tensor(cen[:, :, :], x1, wide(stat[:, 1, :], TB), ALU.add).then_inc(chain, 1)
                dve.wait_ge(chain, c0 + 5)
                dve.tensor_tensor(tmp[:, :, :], cen[:, :, :], cen[:, :, :], ALU.mult).then_inc(chain, 1)
                dve.wait_ge(chain, c0 + 6)
                dve.tensor_reduce(stat[:, 2, :], tmp[:, :, :], AX.X, ALU.add).then_inc(var_done, 1)

            def scale_h1(s):
                dve.wait_ge(std_done, s + 1)
                dve.reciprocal(rstd[:, :], stat[:, 3, :]).then_inc(h1_done, 1)
                dve.wait_ge(h1_done, 2 * s + 1)
                dve.tensor_tensor(h1[:, :, :], cen[:, :, :], wide(rstd[:, :], TB), ALU.mult).then_inc(h1_done, 1)

            def score_bound(s):
                dve.wait_ge(feat_done, s + 1)
                dve.sem_inc(dve_past, 1)
                dve.tensor_reduce(score_max[:, bass.ds(s, 1)], feats_v[:, bass.ds(s * TB, TB), D:FA], AX.XY,
                                  ALU.max, apply_absolute_value=True).then_inc(score_done, 1)

            def strip(s):
                dve.wait_ge(runmax_done, s)
                for c in range(NC):
                    fold_chunk(s, c)
                    if c == 3:
                        search_classes(s - 1)
                        residual(s - 1)
                    if c == 4:
                        scale_h1(s - 1)
                    if c == 6:
                        search_candidates(s - 1)
                dve.wait_ge(runmax_turned, s)
                fold_maxima(s)
                score_bound(s - 1)

            for g in range(NC + 2):
                if g < NC:
                    centre(g)
                if 1 <= g <= NC:
                    variance(g - 1)
                if g >= 2:
                    normalise(g - 2)
                if g >= 3:
                    fold_chunk(0, g - 3)
            constants()
            fold_chunk(0, NC - 1)
            fold_maxima(0)
            dve.wait_ge(x_b2_done, 1)
            with dve.Fori(1, S) as s:
                strip(s)
            residual(S - 1)
            scale_h1(S - 1)
            search_classes(S - 1)
            search_candidates(S - 1)
            score_bound(S - 1)

            dve.wait_ge(top_kept, 2 * S)
            dve.tensor_scalar(gap[:, 1, :], first[:, :], -1.0, MASK, ALU.add, ALU.mult).then_inc(end_chain, 1)
            dve.tensor_scalar(gap[:, 2, :], second[:, :], -1.0, MASK, ALU.add, ALU.mult).then_inc(end_chain, 1)
            dve.wait_ge(end_chain, 2)
            dve.tensor_tensor(gap[:, 3, :], gap[:, 1, :], gap[:, 2, :], ALU.subtract).then_inc(end_chain, 1)
            dve.wait_ge(end_chain, 3)
            dve.tensor_reduce(good[:, 0:1], gap[:, 3, :], AX.X, ALU.min).then_inc(end_chain, 1)
            dve.wait_ge(score_done, S)
            dve.tensor_reduce(good[:, 1:2], score_max[:, :], AX.X, ALU.max).then_inc(end_chain, 1)
            dve.wait_ge(end_chain, 5)
            dve.tensor_scalar(good[:, 2:3], good[:, 0:1], LEAD, None, ALU.is_ge).then_inc(end_chain, 1)
            dve.wait_ge(end_chain, 6)
            dve.scalar_tensor_tensor(good[:, 3:4], good[:, 1:2], HALF_SCORE, good[:, 2:3], ALU.is_le, ALU.mult)\
                .then_inc(good_done, 1)
            dve.wait_ge(good_count, 1)
            dve.tensor_scalar(flag[:, :], ps_hid[0:1, 0:1], P - 0.5, None, ALU.is_lt).then_inc(flag_done, 1)

            for g in range(QG):
                ts = slice(g * OG, (g + 1) * OG)
                dve.wait_ge(got[g], 16 * OG)
                dve.tensor_tensor(gathered[:, ts, :], gathered[:, ts, :],
                                  bias_row[:, :].unsqueeze(1).to_broadcast([P, OG, D]), ALU.add).then_inc(biased, 1)
                dve.wait_ge(biased, g + 1)
                dve.scalar_tensor_tensor(gathered[:, ts, :].rearrange("q t d -> q (t d)"),
                                         gathered[:, ts, :].rearrange("q t d -> q (t d)"), 0.0,
                                         x_tq[:, ts, :].rearrange("q t d -> q (t d)"),
                                         ALU.max, ALU.add).then_inc(out_done, 1)

            dve.wait_ge(flag_done, 1)
            general = dve.value_load(flag[0:1, 0:1], min_val=0, max_val=1)
            with dve.If(general != 0):
                row, neigh, sc = ring[:, 0:N], ring[:, N:2 * N], h_t[:, :]
                for g in range(NB // 4):
                    dve.wait_ge(gen_turned, g + 1)
                    dve.tensor_copy(h_t[0:HEADS, g * W:(g + 1) * W], acc[g % 2][0:HEADS, :]).then_inc(gen_copied, 1)
                dve.wait_ge(out_done, QG)
                dve.wait_ge(stored, 16 * QG)
                dve.sem_inc(gen_head, 1)
                with dve.Fori(0, NB) as ib:
                    dve.wait_ge(gen_row_in, ib * 16 + 16)
                    dve.tensor_scalar(row, row, -1.0, MASK, ALU.add, ALU.mult).then_inc(gen_mask, 1)
                    with dve.Fori(0, HEADS) as h:
                        n = ib * HEADS + h
                        c0 = n * 7
                        dve.wait_ge(gen_neigh_in, n * 16 + 16)
                        dve.tensor_copy(gap[:, 3, 0:1], feats[:, bass.ds(ib * FA + D + h, 1)]).then_inc(gen_chain, 1)
                        dve.wait_ge(gen_chain, c0 + 1)
                        dve.tensor_scalar(sc, neigh, gap[:, 3, 0:1], None, ALU.add).then_inc(gen_chain, 1)
                        dve.wait_ge(gen_chain, c0 + 2)
                        dve.scalar_tensor_tensor(sc, sc, SLOPE, sc, ALU.mult, ALU.max).then_inc(gen_chain, 1)
                        dve.wait_ge(gen_chain, c0 + 3)
                        dve.wait_ge(gen_mask, ib * 2 + 1)
                        dve.tensor_tensor(sc, sc, row, ALU.add).then_inc(gen_chain, 1)
                        dve.wait_ge(gen_chain, c0 + 4)
                        dve.tensor_reduce(gap[:, 0, 0:1], sc, AX.X, ALU.max).then_inc(gen_chain, 1)
                        dve.wait_ge(gen_chain, c0 + 5)
                        dve.tensor_scalar(gap[:, 1, 0:1], gap[:, 0, 0:1], -1.0, None, ALU.mult).then_inc(gen_max, 1)
                        for g in range(NB // 4):
                            dve.wait_ge(gen_p_turned, n * (NB // 4) + g + 1)
                            dve.tensor_copy(max_lo[:, (g % 2) * W:(g % 2 + 1) * W], acc[g % 2][:, :])\
                                .then_inc(gen_p_copied, 1)
                        dve.wait_ge(gen_exp, n + 1)
                        dve.reciprocal(gap[:, 3, 1:2], gap[:, 2, 0:1]).then_inc(gen_chain, 1)
                        dve.wait_ge(gen_chain, c0 + 6)
                        dve.wait_ge(gen_sum, n + 1)
                        dve.tensor_scalar(cen[:, 0:1, :].rearrange("q a d -> q (a d)")[:, bass.ds(h * HD, HD)],
                                          ps_hid[:, 0:HD], gap[:, 3, 1:2], None, ALU.mult).then_inc(gen_chain, 1)
                        dve.wait_ge(gen_chain, c0 + 7)
                        dve.sem_inc(gen_head, 1)
                    dve.tensor_tensor(h1[:, 0, :], cen[:, 0, :], bias_row[:, :], ALU.add).then_inc(gen_mask, 1)
                    dve.wait_ge(gen_mask, ib * 2 + 2)
                    dve.scalar_tensor_tensor(tmp[:, 0, :], h1[:, 0, :], 0.0,
                                             x_tq[:, bass.ds(ib, 1), :].rearrange("q a d -> q (a d)"),
                                             ALU.max, ALU.add).then_inc(gen_out, 1)

        @block.tensor
        def _(pe):
            def turn_first(g):
                pe.wait_ge(pro_norm, g + 1)
                if g:
                    pe.wait_ge(pro_h, 2 * g)
                for k in range(CB):
                    last = pe.transpose(pro_banks[k // 4][:, k % 4, :], x_pb[:, g * CB + k, :], ident[:, :])
                last.then_inc(pro_turned, 1)

            def products(s, c, parity):
                pe.wait_ge(chunk_in[c % RING], s * (16 * NC // RING) + 16 * (c // RING + 1))
                for b in range(CB):
                    at = (b % 2) * D
                    last = pe.matmul(acc[parity][at:at + D, :], x_pb[:, c * CB + b, :], slot(c)[:, b * W:(b + 1) * W],
                                     start=(c == 0 and b < 2), stop=(c == NC - 1 and b >= CB - 2))
                return last

            def sums(c):
                for b in range(CB):
                    at = (b % 4) * QUAD
                    last = pe.matmul(row_sums[at:at + QUAD, :], ones_cols[:, :], slot(c)[:, b * W:(b + 1) * W],
                                     start=(c == 0 and b < 4), stop=(c == NC - 1 and b >= CB - 4))
                return last

            def chunk(s, c, parity, first=False):
                if c % 2:
                    pe.wait_ge(chunk_in[c % RING], s * (16 * NC // RING) + 16 * (c // RING + 1))
                    sums(c)
                last = products(s, c, parity)
                if c % 2 == 0:
                    if c == 0 and not first:
                        pe.wait_ge(rows_copied, s)
                    last = sums(c)
                last.then_inc(pe_chunk, 1)

            def mlp_hidden(s):
                pe.wait_ge(strip_h_done, s + 1)
                pe.matmul(ps_hid[:, :], w1_sb[:, :], h_strip[:, :], start=True, stop=True).then_inc(hid_ready, 1)

            def turn_sums(s):
                pe.wait_ge(rows_copied, s + 1)
                pe.wait_ge(acc_copied, s + 1)
                pe.wait_ge(hid_done, s + 1)
                for k in range(TB):
                    at = slice(k * P, (k + 1) * P)
                    pe.matmul(ps_acc[:, k, 0:D], acc_sb[:, at], b_t_twice[:, :], start=True, stop=False)
                    pe.matmul(ps_acc[:, k, 0:D], hidden[:, at], w2_sb[:, :], start=False, stop=True)
                    pe.matmul(ps_acc[:, k, D:D + 1], row_sb[:, at], fold_rows[:, :], start=True, stop=True)
                for k in range(TB):
                    last = pe.matmul(ps_xb[:, k, :], h_strip[:, k * P:(k + 1) * P], b_t_twice[0:D, :],
                                     start=True, stop=True)
                last.then_inc(acc_turned, 1)

            def turn_maxima(s):
                pe.wait_ge(runmax_done, s + 1)
                for k in range(TB):
                    last = pe.transpose(ps_turn[:, k * P:(k + 1) * P], runmax[:, k * P:(k + 1) * P], ident[:, :])
                last.then_inc(runmax_turned, 1)

            def turn_h1(s, bank):
                pe.wait_ge(h1_done, 2 * s + 2)
                pe.sem_inc(pe_past, 1)
                for k in range(TB):
                    last = pe.transpose(bank[0:D, k * P:(k + 1) * P], h1[:, k, :], ident[:, :])
                last.then_inc(h1_turned, 1)

            def features(s):
                pe.wait_ge(h1_t_done, s + 1)
                for k in range(TB):
                    last = pe.matmul(ps_feat[:, k, :], h1_t[:, k * P:(k + 1) * P], w_ext[:, :],
                                     start=True, stop=True)
                last.then_inc(feat_ready, 1)

            def strip(s, parity):
                for c in range(NC):
                    if c == 1:
                        turn_maxima(s - 1)
                        turn_sums(s - 1)
                    chunk(s, c, parity)
                    if c == 3:
                        turn_h1(s - 1, ps_turn)
                    if c == 4:
                        features(s - 1)
                    if c == 5:
                        mlp_hidden(s)

            for c in range(NC):
                pe.wait_ge(pro_norm, c + 1)
                chunk(0, c, 0, first=True)
                if c == 0:
                    pe.wait_ge(pool_const, 9)
                turn_first(c)
            pe.wait_ge(dve_const, 2)
            pe.matmul(ps_feat[0:D, 0, 0:2 * HEADS], w_gat_t_sb[:, :], att_diag[:, :],
                      start=True, stop=True).then_inc(w_ext_ready, 1)
            pe.wait_ge(w_ext_done, 1)
            mlp_hidden(0)
            with pe.Fori(0, S // 2 - 1) as r:
                strip(2 * r + 1, 1)
                strip(2 * r + 2, 0)
            strip(S - 1, 1)
            turn_maxima(S - 1)
            turn_sums(S - 1)
            turn_h1(S - 1, ps_hid)
            features(S - 1)
            pe.wait_ge(good_done, 1)
            pe.matmul(ps_hid[0:1, 0:1], good[:, 3:4], ones[:, :], start=True, stop=True).then_inc(good_count, 1)

            pe.wait_ge(flag_done, 1)
            general = pe.value_load(flag[0:1, 0:1], min_val=0, max_val=1)
            with pe.If(general != 0):
                for g in range(NB // 4):
                    if g >= 2:
                        pe.wait_ge(gen_copied, g - 1)
                    for k in range(4):
                        last = pe.transpose(acc[g % 2][0:HEADS, k * P:(k + 1) * P],
                                            feats_v[:, g * 4 + k, D + HEADS:FA], ident[:, :])
                    last.then_inc(gen_turned, 1)
                with pe.Fori(0, NB) as ib:
                    with pe.Fori(0, HEADS) as h:
                        n = ib * HEADS + h

                        def turn(g):
                            if g >= 2:
                                pe.wait_ge(gen_p_copied, n * (NB // 4) + g - 1)
                            for k in range(4):
                                j = g * 4 + k
                                last = pe.transpose(acc[g % 2][:, k * P:(k + 1) * P],
                                                    h_t[:, j * P:(j + 1) * P], ident[:, :])
                            last.then_inc(gen_p_turned, 1)

                        pe.wait_ge(gen_exp, n + 1)
                        turn(0)
                        for g in range(NB // 4):
                            if g + 1 < NB // 4:
                                turn(g + 1)
                            pe.wait_ge(gen_p_copied, n * (NB // 4) + g + 1)
                            for k in range(4):
                                j = g * 4 + k
                                at = (g % 2) * W + k * P
                                last = pe.matmul(ps_hid[:, 0:HD], max_lo[:, at:at + P],
                                                 feats[:, bass.ds(h * HD + j * FA, HD)],
                                                 start=(j == 0), stop=(j == NB - 1))
                        last.then_inc(gen_sum, 1)


def kernel(x, adj, L0_gnn_t, L0_gnn_B, L0_gnn_W1, L0_gnn_b1, L0_gnn_W2, L0_gnn_b2,
           L1_gnn_W, L1_gnn_att_self, L1_gnn_att_neigh, L1_gnn_bias):
    import numpy as np
    import concourse.bacc as bacc
    from concourse.bass_utils import run_bass_kernel_spmd

    adj = np.asarray(adj)
    w1 = np.asarray(L0_gnn_W1)
    w_gat = np.asarray(L1_gnn_W)
    tiles = adj.reshape(S, W, P, NC, CB).transpose(0, 3, 2, 4, 1)
    arrays = {
        "x": x,
        "adj": adj,
        "adj_t": tiles.reshape(S * NC, P, CB * W),
        "w1": w1[0:D],
        "w1_t": w1[D:D + 1].reshape(HID, 1),
        "b1": np.asarray(L0_gnn_b1).reshape(HID, 1),
        "t_in": np.asarray(L0_gnn_t).reshape(1, 1),
        "w2": L0_gnn_W2,
        "b2": np.asarray(L0_gnn_b2).reshape(1, D),
        "b_t": np.asarray(L0_gnn_B).T,
        "w_gat": w_gat,
        "w_gat_t": w_gat.T,
        "att_self": np.asarray(L1_gnn_att_self).reshape(D, 1),
        "att_neigh": np.asarray(L1_gnn_att_neigh).reshape(D, 1),
        "bias": np.asarray(L1_gnn_bias).reshape(1, D),
    }
    nc = bacc.Bacc("TRN2", target_bir_lowering=False, num_devices=1)
    arrays = {f"in_{n}": np.ascontiguousarray(a) for n, a in arrays.items()}
    ins = [nc.dram_tensor(n, a.shape, mybir.dt.from_np(a.dtype), kind="ExternalInput").ap() for n, a in arrays.items()]
    out = nc.dram_tensor("out", (N, D), F32, kind="ExternalOutput").ap()
    build(nc, *ins, out)
    r = run_bass_kernel_spmd(nc, [arrays], core_ids=[0])
    return r.results[0]["out"]
```

```python
from contextlib import ExitStack

import concourse.bass as bass
from concourse import mybir

F32 = mybir.dt.float32
I32 = mybir.dt.int32
U32 = mybir.dt.uint32
ALU = mybir.AluOpType
ACT = mybir.ActivationFunctionType
AX = mybir.AxisListType

P = 128
N = 8192
D = 64
HID = 128
HEADS, HD = 8, 8
NB = N // P
W = 512
S = N // W
TB = W // P
CB = 8
NC = NB // CB
RING = 4
HALF = CB * W // 2
QUAD = 32
FA = D + 2 * HEADS
EPS = 1e-5
SLOPE = 0.2
MASK = 1e10
LEAD = 505.0
HALF_SCORE = 50.0
OG = 8
QG = NB // OG


def build(nc, x, adj, adj_t, w1, w1_t, b1, t_in, w2, b2, b_t, w_gat, w_gat_t, att_self, att_neigh, bias, out):
    with ExitStack() as ctx:
        def sb(name, shape, dt=F32):
            return ctx.enter_context(nc.sbuf_tensor(name, shape, dt))

        def pb(name, shape, dt=F32):
            return ctx.enter_context(nc.psum_tensor(name, shape, dt))

        def sem(name):
            return ctx.enter_context(nc.semaphore(name))

        feats_dram = nc.dram_tensor("feats_dram", (N, D), F32, kind="Internal").ap()
        neigh_dram = nc.dram_tensor("neigh_dram", (HEADS, N), F32, kind="Internal").ap()

        ring = sb("ring", [P, RING * CB * W])
        gathered = sb("gathered", [P, NB, D])
        ones_cols = sb("ones_cols", [P, QUAD])
        h_t = sb("h_t", [P, N])
        x_pb = sb("x_pb", [P, NB, D])
        x_tq = sb("x_tq", [P, NB, D])
        feats = sb("feats", [P, NB * FA])
        max_lo = sb("max_lo", [P, HALF])
        max_hi = sb("max_hi", [P, HALF])
        cand = sb("cand", [P, TB, NB])
        hidden = sb("hidden", [HID, W])
        acc_sb = sb("acc_sb", [P, W])
        row_sb = sb("row_sb", [P, W])
        acc_tq = sb("acc_tq", [P, TB, D + 1])
        tmp = sb("tmp", [P, TB, D])
        cen = sb("cen", [P, TB, D])
        h1 = sb("h1", [P, TB, D])
        h1_t = sb("h1_t", [P, W // 2])
        h_strip = sb("h_strip", [P, W // 2])
        stat = sb("stat", [P, 4, TB])
        rstd = sb("rstd", [P, TB])
        squares = [acc_sb, row_sb]
        pstat = sb("pstat", [P, 5, NB])
        ident = sb("ident", [P, P])
        b_t_twice = sb("b_t_twice", [P, D])
        b_t_diag = sb("b_t_diag", [P, 2 * D])
        w1_sb = sb("w1_sb", [P, 2 * HID])
        w2_sb = sb("w2_sb", [HID, D])
        hid_bias = sb("hid_bias", [HID, 4])
        b2_row = sb("b2_row", [P, D])
        fold_rows = sb("fold_rows", [P, D])
        w_ext = sb("w_ext", [P, 2 * FA])
        w_gat_t_sb = sb("w_gat_t_sb", [D, D])
        att_diag = sb("att_diag", [D, 2 * HEADS])
        att_col = sb("att_col", [D, 2])
        head_mask = sb("head_mask", [D, HEADS])
        bias_row = sb("bias_row", [P, D])
        eps = sb("eps", [P, 1])
        ones = sb("ones", [P, 1])
        node = sb("node", [P, NB], I32)
        runmax = sb("runmax", [P, W])
        top_cls = sb("top_cls", [P, TB, 8])
        idx_cls = sb("idx_cls", [P, TB, 8], U32)
        top_cand = sb("top_cand", [P, TB, 8])
        idx_cand = sb("idx_cand", [P, TB, 8], U32)
        cls_row = sb("cls_row", [P, TB], U32)
        first = sb("first", [P, NB])
        second = sb("second", [P, NB])
        best = sb("best", [P, NB], U32)
        gap = sb("gap", [P, 4, NB])
        good = sb("good", [P, 4])
        flag = sb("flag", [1, 1], I32)

        acc = [pb(f"acc{i}", [P, W]) for i in range(2)]
        row_sums = pb("row_sums", [P, W])
        ps_hid = pb("ps_hid", [P, W])
        ps_acc = pb("ps_acc", [P, TB, 2 * D])
        ps_xb = pb("ps_xb", [P, TB, D])
        ps_turn = pb("ps_turn", [P, W])
        ps_feat = pb("ps_feat", [P, TB, FA])

        consts_in = sem("consts_in")
        att_in = sem("att_in")
        x_b2_done = sem("x_b2_done")
        x_in = [sem(f"x_in{k}") for k in range(2)]
        x_tq_in = sem("x_tq_in")
        pool_const = sem("pool_const")
        dve_const = sem("dve_const")
        w_ext_ready = sem("w_ext_ready")
        w_ext_done = sem("w_ext_done")
        pro_chain = sem("pro_chain")
        pro_centred = sem("pro_centred")
        pro_squared = sem("pro_squared")
        pro_var = sem("pro_var")
        pro_recip = sem("pro_recip")
        pro_std = sem("pro_std")
        pro_norm = sem("pro_norm")
        pro_turned = sem("pro_turned")
        pro_h = sem("pro_h")
        chunk_in = [sem(f"chunk_in{r}") for r in range(RING)]
        pe_chunk = sem("pe_chunk")
        lo_done = sem("lo_done")
        hi_done = sem("hi_done")
        fold = sem("fold")
        hid_ready = sem("hid_ready")
        hid_done = sem("hid_done")
        strip_h_done = sem("strip_h_done")
        acc_copied = sem("acc_copied")
        rows_copied = sem("rows_copied")
        acc_turned = sem("acc_turned")
        acc_tq_done = sem("acc_tq_done")
        chain = sem("chain")
        x1_done = sem("x1_done")
        var_done = sem("var_done")
        std_done = sem("std_done")
        h1_done = sem("h1_done")
        h1_turned = sem("h1_turned")
        h1_t_done = sem("h1_t_done")
        feat_ready = sem("feat_ready")
        feat_done = sem("feat_done")
        feat_stored = sem("feat_stored")
        runmax_done = sem("runmax_done")
        runmax_turned = sem("runmax_turned")
        cls_top = sem("cls_top")
        cls_done = sem("cls_done")
        cls_row_done = sem("cls_row_done")
        cand_in = sem("cand_in")
        cand_top = sem("cand_top")
        cand_done = sem("cand_done")
        top_kept = sem("top_kept")
        best_done = sem("best_done")
        got = [sem(f"got{g}") for g in range(QG)]
        end_chain = sem("end_chain")
        good_done = sem("good_done")
        good_count = sem("good_count")
        flag_done = sem("flag_done")
        biased = sem("biased")
        out_done = sem("out_done")
        stored = sem("stored")
        sp_past = sem("sp_past")
        pool_past = sem("pool_past")
        dve_past = sem("dve_past")
        pe_past = sem("pe_past")
        gen_turned = sem("gen_turned")
        gen_copied = sem("gen_copied")
        gen_neigh_stored = sem("gen_neigh_stored")
        gen_row_in = sem("gen_row_in")
        gen_neigh_in = sem("gen_neigh_in")
        gen_chain = sem("gen_chain")
        gen_mask = sem("gen_mask")
        gen_max = sem("gen_max")
        gen_exp = sem("gen_exp")
        gen_p_turned = sem("gen_p_turned")
        gen_p_copied = sem("gen_p_copied")
        gen_sum = sem("gen_sum")
        gen_head = sem("gen_head")
        gen_out = sem("gen_out")
        gen_stored = sem("gen_stored")

        x_by_p = x.rearrange("(p b) d -> p b d", b=NB)
        x_by_q = x.rearrange("(s q k) d -> q s (k d)", q=P, k=TB)
        out_by_q = out.rearrange("(s q k) d -> q s (k d)", q=P, k=TB)
        feats_by_q = feats_dram.rearrange("(s q k) d -> q s (k d)", q=P, k=TB)
        classes = adj.rearrange("i (p b) -> (i p) b", b=NB)
        h_by_block = h_t[0:D, :].rearrange("d (k p m) -> d m k p", k=TB, p=P)
        h_by_k = h_t[0:D, :].rearrange("d (k n) -> d k n", k=TB)
        feats_v = feats[:, :].rearrange("q (t f) -> q t f", f=FA)
        pro_banks = [ps_turn[0:D, :].rearrange("d (k q) -> d k q", q=P),
                     ps_acc[0:D, :, :]]

        def slot(n):
            return ring[:, (n % RING) * CB * W:(n % RING + 1) * CB * W]

        def wide(a, k, n=D):
            return a.unsqueeze(2).to_broadcast([P, k, n])

        block = ctx.enter_context(nc.Block())

        @block.sync
        def _(sp):
            for k, (b0, b1_) in enumerate(((0, 2 * CB), (2 * CB, NB))):
                sp.dma_start(x_pb[:, b0:b1_, :], x_by_p[:, b0:b1_, :]).then_inc(x_in[k], 16)
            for n in range(RING):
                sp.dma_start(slot(n), adj_t[n]).then_inc(chunk_in[n % RING], 16)
            sp.dma_start(x_tq[:, :, :].rearrange("q (s k) d -> q s (k d)", k=TB), x_by_q).then_inc(x_tq_in, 16)

            def load(s, c):
                sp.wait_ge(pe_chunk, s * NC + (c - RING + 1))
                sp.wait_ge(hi_done, s * NC + (c - RING + 1))
                sp.sem_inc(sp_past, 1)
                src = adj_t[bass.ds(s * NC + c, 1)].rearrange("a p f -> (a p) f")
                sp.dma_start(slot(c), src).then_inc(chunk_in[c % RING], 16)

            def store_feats(s):
                sp.wait_ge(feat_done, s + 1)
                sp.sem_inc(sp_past, 1)
                dst = feats_by_q[:, bass.ds(s, 1), :].rearrange("q a (k d) -> q (a k) d", d=D)
                sp.dma_start(dst, feats_v[:, bass.ds(s * TB, TB), 0:D]).then_inc(feat_stored, 16)

            for c in range(RING, NC):
                load(0, c)
            with sp.Fori(1, S) as s:
                for c in range(NC):
                    load(s, c)
                store_feats(s - 1)
            store_feats(S - 1)
            for g in range(QG):
                sp.wait_ge(out_done, g + 1)
                ts = slice(g * OG, (g + 1) * OG)
                sp.dma_start(out_by_q[:, g * OG // TB:(g + 1) * OG // TB, :],
                             gathered[:, ts, :].rearrange("q (s k) d -> q s (k d)", k=TB)).then_inc(stored, 16)
            sp.wait_ge(stored, 16 * QG)

            sp.wait_ge(flag_done, 1)
            general = sp.value_load(flag[0:1, 0:1], min_val=0, max_val=1)
            with sp.If(general != 0):
                sp.wait_ge(gen_copied, NB // 4)
                sp.dma_start(neigh_dram, h_t[0:HEADS, :]).then_inc(gen_neigh_stored, 16)
                sp.wait_ge(gen_neigh_stored, 16)
                adj_rows = adj.rearrange("(s q k) j -> s k q j", q=P, k=TB)
                out_rows = out.rearrange("(s q k) d -> s k q d", q=P, k=TB)
                with sp.Fori(0, S) as s:
                    for k in range(TB):
                        ib = s * TB + k
                        sp.wait_ge(gen_head, s * (TB * HEADS) + (k * HEADS + 1))
                        sp.sem_inc(sp_past, 1)
                        sp.dma_start(ring[:, 0:N], adj_rows[bass.ds(s, 1), k].rearrange("a q j -> (a q) j"))\
                            .then_inc(gen_row_in, 16)
                        with sp.Fori(0, HEADS) as h:
                            sp.wait_ge(gen_head, ib * HEADS + h + 1)
                            sp.sem_inc(sp_past, 1)
                            sp.dma_start(ring[:, N:2 * N], neigh_dram[bass.ds(h, 1), :].to_broadcast([P, N]))\
                                .then_inc(gen_neigh_in, 16)
                        sp.wait_ge(gen_out, s * TB + (k + 1))
                        sp.sem_inc(sp_past, 1)
                        sp.dma_start(out_rows[bass.ds(s, 1), k].rearrange("a q d -> (a q) d"), tmp[:, 0, :])\
                            .then_inc(gen_stored, 16)
                        sp.wait_ge(gen_stored, s * (16 * TB) + (k * 16 + 16))
                        sp.sem_inc(sp_past, 1)

        @block.gpsimd
        def _(pool):
            for n, (dst, value) in enumerate(((ones[:, :], 1.0), (eps[:, :], EPS), (ones_cols[:, :], 1.0),
                                              (head_mask[:, :], 1.0), (b_t_diag[:, :], 0.0), (w_ext[:, :], 0.0), (w1_sb[:, :], 0.0),
                                              (ident[:, :], 0.0))):
                pool.memset(dst, value).then_inc(pool_const, 1)
                pool.wait_ge(pool_const, n + 1)
            pool.affine_select(out=ident[:, :], in_=ident[:, :], compare_op=ALU.not_equal, fill=1.0,
                               base=0, pattern=[[-1, P]], channel_multiplier=1).then_inc(pool_const, 1)
            pool.wait_ge(pool_const, 9)
            pool.affine_select(out=head_mask[:, :], in_=head_mask[:, :], compare_op=ALU.is_ge, fill=0.0,
                               base=0, pattern=[[-HD, HEADS]], channel_multiplier=1).then_inc(pool_const, 1)
            pool.wait_ge(pool_const, 10)
            pool.affine_select(out=head_mask[:, :], in_=head_mask[:, :], compare_op=ALU.is_ge, fill=0.0,
                               base=HD - 1, pattern=[[HD, HEADS]], channel_multiplier=-1)\
                .then_inc(pool_const, 1)
            pool.wait_ge(pool_const, 11)
            pool.iota(node[:, :].rearrange("q (s k) -> q s k", k=TB), pattern=[[W, S], [1, TB]], base=0,
                      channel_multiplier=TB)\
                .then_inc(pool_const, 1)

            pool.wait_ge(consts_in, 16 * 15)
            pool.wait_ge(x_tq_in, 16)
            pool.tensor_tensor(x_tq[:, :, :], x_tq[:, :, :], b2_row[:, :].unsqueeze(1).to_broadcast([P, NB, D]),
                               ALU.add).then_inc(x_b2_done, 1)

            with pool.Fori(0, S) as s:
                pool.wait_ge(cls_row_done, s + 1)
                pool.sem_inc(pool_past, 1)
                for k in range(TB):
                    pool.indirect_dma_start(
                        out=cand[:, k, :], out_offset=None, in_=classes,
                        in_offset=bass.IndirectOffsetOnAxis(ap=cls_row[:, k:k + 1], axis=0),
                    ).then_inc(cand_in, 16)
            pool.wait_ge(feat_stored, 16 * S)
            pool.wait_ge(best_done, S - 1)
            for t in range(NB):
                if t == NB - TB:
                    pool.wait_ge(best_done, S)
                pool.indirect_dma_start(
                    out=gathered[:, t, :], out_offset=None, in_=feats_dram,
                    in_offset=bass.IndirectOffsetOnAxis(ap=best[:, t:t + 1], axis=0),
                ).then_inc(got[t // OG], 16)

        @block.scalar
        def _(act):
            act.wait_ge(pool_const, 12)

            def load_weights():
                for dst, src in ((w_gat_t_sb[:, :], w_gat_t), (w1_sb[0:D, 0:HID], w1), (w1_sb[D:P, HID:2 * HID], w1), (w2_sb[:, :], w2),
                                 (hid_bias[:, 0:1], b1), (hid_bias[:, 1:2], w1_t),
                                 (hid_bias[:, 2:3], t_in.to_broadcast([HID, 1])),
                                 (b_t_twice[0:D, :], b_t), (b_t_twice[D:P, :], b_t),
                                 (b_t_diag[0:D, 0:D], b_t), (b_t_diag[D:P, D:2 * D], b_t),
                                 (b2_row[:, :], b2.to_broadcast([P, D])),
                                 (w_ext[0:D, 0:D], w_gat), (w_ext[D:P, FA:FA + D], w_gat), (bias_row[:, :], bias.to_broadcast([P, D]))):
                    act.dma_start(dst, src).then_inc(consts_in, 16)
                act.dma_start(att_col[:, 0:1], att_self).then_inc(att_in, 16)
                act.dma_start(att_col[:, 1:2], att_neigh).then_inc(att_in, 16)

            def square(g):
                act.wait_ge(pro_centred, g + 1)
                if g >= 2:
                    act.wait_ge(pro_var, g - 1)
                act.activation(squares[g % 2][:, :], x_pb[:, g * CB:(g + 1) * CB, :].rearrange("p b d -> p (b d)"),
                               ACT.Square).then_inc(pro_squared, 1)

            def deviation(g):
                act.wait_ge(pro_var, g + 1)
                act.activation(pstat[:, 3, g * CB:(g + 1) * CB], pstat[:, 2, g * CB:(g + 1) * CB], ACT.Sqrt,
                               bias=eps[:, :], scale=1.0 / D).then_inc(pro_std, 1)

            def place(g):
                act.wait_ge(pro_turned, g + 1)
                for half, src in enumerate(pro_banks):
                    act.copy(h_by_block[:, g * (CB // TB) + half], src).then_inc(pro_h, 1)

            for g in range(NC + 2):
                if g < NC:
                    square(g)
                if g >= 2:
                    place(g - 2)
                if g < NC:
                    deviation(g)
                if g == 0:
                    load_weights()
            act.wait_ge(w_ext_ready, 1)
            for k in range(2):
                half = slice(k * D, (k + 1) * D)
                act.copy(w_ext[half, k * FA + D:(k + 1) * FA], ps_feat[half, 0, 0:2 * HEADS]).then_inc(w_ext_done, 1)

            def tanh(s):
                act.wait_ge(hid_ready, s + 1)
                act.activation(hidden[:, :], ps_hid[:, :], ACT.Tanh, bias=hid_bias[:, 3:4])\
                    .then_inc(hid_done, 1)

            def strip_h(s):
                for k in range(2):
                    act.copy(h_strip[k * D:(k + 1) * D, :].rearrange("d (m q) -> d m q", q=P),
                             h_by_k[:, 2 * k:2 * k + 2, bass.ds(s * P, P)]).then_inc(strip_h_done, 1)

            def finish_strip(s, parity, last=False):
                act.wait_ge(pe_chunk, s * NC + NC)
                act.copy(acc_sb[:, :], acc[parity][:, :]).then_inc(acc_copied, 1)
                act.copy(row_sb[:, :], row_sums[:, :]).then_inc(rows_copied, 1)
                act.wait_ge(acc_turned, s + 1)
                act.copy(acc_tq[:, :, :], ps_acc[:, :, 0:D + 1]).then_inc(acc_tq_done, 1)
                if not last:
                    strip_h(s + 1)
                act.wait_ge(var_done, s + 1)
                act.activation(stat[:, 3, :], stat[:, 2, :], ACT.Sqrt, bias=eps[:, :], scale=1.0 / D)\
                    .then_inc(std_done, 1)
                act.wait_ge(h1_turned, s + 1)
                act.activation(h1_t[:, :], (ps_hid if last else ps_turn)[:, 0:W // 2], ACT.Relu).then_inc(h1_t_done, 1)
                act.wait_ge(feat_ready, s + 1)
                act.copy(feats[:, bass.ds(s * (TB * FA), TB * FA)],
                         ps_feat[:, :, :].rearrange("q t f -> q (t f)")).then_inc(feat_done, 1)

            act.wait_ge(pro_h, 2 * NC)
            strip_h(0)
            act.wait_ge(dve_const, 4)
            tanh(0)
            with act.Fori(0, S // 2 - 1) as r:
                for k in range(2):
                    finish_strip(2 * r + k, k)
                    tanh(2 * r + k + 1)
            finish_strip(S - 2, 0)
            tanh(S - 1)
            finish_strip(S - 1, 1, last=True)

            act.wait_ge(flag_done, 1)
            general = act.value_load(flag[0:1, 0:1], min_val=0, max_val=1)
            with act.If(general != 0):
                with act.Fori(0, NB * HEADS) as n:
                    act.wait_ge(gen_max, n + 1)
                    act.activation(h_t[:, :], h_t[:, :], ACT.Exp, bias=gap[:, 1, 0:1], accum_out=gap[:, 2, 0:1])\
                        .then_inc(gen_exp, 1)

        @block.vector
        def _(dve):
            def constants():
                dve.wait_ge(consts_in, 16 * 15)
                dve.wait_ge(att_in, 32)
                dve.wait_ge(pool_const, 12)
                for k in range(2):
                    dve.tensor_scalar(att_diag[:, k * HEADS:(k + 1) * HEADS], head_mask[:, :], att_col[:, k:k + 1],
                                      None, ALU.mult).then_inc(dve_const, 1)
                dve.tensor_tensor(hid_bias[:, 3:4], hid_bias[:, 1:2], hid_bias[:, 2:3], ALU.mult)\
                    .then_inc(dve_const, 1)
                dve.wait_ge(dve_const, 3)
                dve.tensor_tensor(hid_bias[:, 3:4], hid_bias[:, 3:4], hid_bias[:, 0:1], ALU.add)\
                    .then_inc(dve_const, 1)
                dve.tensor_reduce(pstat[:, 0, 0:1], ident[:, :].rearrange("p (a b) -> p b a", b=QUAD)[:, 0, :], AX.X, ALU.add)\
                    .then_inc(dve_const, 1)
                dve.wait_ge(dve_const, 5)
                dve.tensor_copy(fold_rows[:, :], pstat[:, 0, 0:1].to_broadcast([P, D])).then_inc(dve_const, 1)

            def centre(g):
                b = slice(g * CB, (g + 1) * CB)
                dve.wait_ge(x_in[g >= 2], 16)
                dve.tensor_reduce(pstat[:, 0, b], x_pb[:, b, :], AX.X, ALU.add).then_inc(pro_chain, 1)
                dve.wait_ge(pro_chain, 2 * g + 1)
                dve.tensor_scalar(pstat[:, 1, b], pstat[:, 0, b], -1.0 / D, None, ALU.mult).then_inc(pro_chain, 1)
                dve.wait_ge(pro_chain, 2 * g + 2)
                dve.tensor_tensor(x_pb[:, b, :], x_pb[:, b, :], wide(pstat[:, 1, b], CB), ALU.add)\
                    .then_inc(pro_centred, 1)

            def variance(g):
                b = slice(g * CB, (g + 1) * CB)
                dve.wait_ge(pro_squared, g + 1)
                dve.tensor_reduce(pstat[:, 2, b], squares[g % 2][:, :].rearrange("p (b d) -> p b d", d=D),
                                  AX.X, ALU.add).then_inc(pro_var, 1)

            def normalise(g):
                b = slice(g * CB, (g + 1) * CB)
                dve.wait_ge(pro_std, g + 1)
                dve.reciprocal(pstat[:, 4, b], pstat[:, 3, b]).then_inc(pro_recip, 1)
                dve.wait_ge(pro_recip, g + 1)
                dve.scalar_tensor_tensor(x_pb[:, b, :], x_pb[:, b, :], 0.0, wide(pstat[:, 4, b], CB),
                                         ALU.max, ALU.mult).then_inc(pro_norm, 1)

            def fold_chunk(s, c):
                n = s * NC + c
                dve.wait_ge(chunk_in[c % RING], s * (16 * NC // RING) + 16 * (c // RING + 1))
                lo, hi = slot(c)[:, 0:HALF], slot(c)[:, HALF:2 * HALF]
                if c == 0:
                    dve.tensor_tensor(max_lo[:, :], lo, hi, ALU.max).then_inc(hi_done, 1)
                elif c == 1:
                    dve.tensor_tensor(max_hi[:, :], lo, hi, ALU.max).then_inc(hi_done, 1)
                else:
                    dve.wait_ge(hi_done, n)
                    dve.tensor_tensor(max_lo[:, :], max_lo[:, :], lo, ALU.max).then_inc(lo_done, 1)
                    dve.tensor_tensor(max_hi[:, :], max_hi[:, :], hi, ALU.max).then_inc(hi_done, 1)

            def fold_maxima(s):
                dve.wait_ge(hi_done, s * NC + NC)
                dve.wait_ge(lo_done, s * (NC - 2) + NC - 2)
                dve.tensor_tensor(max_lo[:, :], max_lo[:, :], max_hi[:, :], ALU.max).then_inc(fold, 1)
                dve.wait_ge(fold, s * 2 + 1)
                dve.tensor_tensor(max_lo[:, 0:2 * W], max_lo[:, 0:2 * W], max_lo[:, 2 * W:4 * W], ALU.max)\
                    .then_inc(fold, 1)
                dve.wait_ge(fold, s * 2 + 2)
                dve.tensor_tensor(runmax[:, :], max_lo[:, 0:W], max_lo[:, W:2 * W], ALU.max)\
                    .then_inc(runmax_done, 1)

            def search_classes(s):
                ts = bass.ds(s * TB, TB)
                dve.wait_ge(runmax_turned, s + 1)
                dve.sem_inc(dve_past, 1)
                for k in range(TB):
                    dve.max(top_cls[:, k, :], ps_turn[:, k * P:(k + 1) * P]).then_inc(cls_top, 1)
                dve.wait_ge(cls_top, s * TB + TB)
                dve.sem_inc(dve_past, 1)
                for k in range(TB):
                    dve.max_index(idx_cls[:, k, :], top_cls[:, k, :], ps_turn[:, k * P:(k + 1) * P])\
                        .then_inc(cls_done, 1)
                dve.tensor_copy(first[:, ts], top_cls[:, :, 0]).then_inc(top_kept, 1)
                dve.wait_ge(cls_done, s * TB + TB)
                dve.scalar_tensor_tensor(cls_row[:, :], node[:, ts], float(P), idx_cls[:, :, 0], ALU.mult, ALU.add)\
                    .then_inc(cls_row_done, 1)

            def search_candidates(s):
                ts = bass.ds(s * TB, TB)
                dve.wait_ge(cand_in, s * (16 * TB) + 16 * TB)
                dve.sem_inc(dve_past, 1)
                for k in range(TB):
                    dve.max(top_cand[:, k, :], cand[:, k, :]).then_inc(cand_top, 1)
                dve.wait_ge(cand_top, s * TB + TB)
                dve.sem_inc(dve_past, 1)
                for k in range(TB):
                    dve.max_index(idx_cand[:, k, :], top_cand[:, k, :], cand[:, k, :]).then_inc(cand_done, 1)
                dve.tensor_tensor(second[:, ts], top_cls[:, :, 1], top_cand[:, :, 1], ALU.max)\
                    .then_inc(top_kept, 1)
                dve.wait_ge(cand_done, s * TB + TB)
                dve.scalar_tensor_tensor(best[:, ts], idx_cls[:, :, 0], float(NB), idx_cand[:, :, 0],
                                         ALU.mult, ALU.add).then_inc(best_done, 1)

            def residual(s):
                x1 = x_tq[:, bass.ds(s * TB, TB), :]
                c0 = s * 6
                dve.wait_ge(acc_tq_done, s + 1)
                dve.tensor_tensor(tmp[:, :, :], ps_xb[:, :, :],
                                  acc_tq[:, :, D:D + 1].to_broadcast([P, TB, D]), ALU.mult).then_inc(chain, 1)
                dve.wait_ge(chain, c0 + 1)
                dve.tensor_tensor(tmp[:, :, :], acc_tq[:, :, 0:D], tmp[:, :, :], ALU.subtract).then_inc(chain, 1)
                dve.wait_ge(chain, c0 + 2)
                dve.tensor_tensor(x1, x1, tmp[:, :, :], ALU.add).then_inc(x1_done, 1)
                dve.wait_ge(x1_done, s + 1)
                dve.sem_inc(dve_past, 1)
                dve.tensor_reduce(stat[:, 0, :], x1, AX.X, ALU.add).then_inc(chain, 1)
                dve.wait_ge(chain, c0 + 3)
                dve.tensor_scalar(stat[:, 1, :], stat[:, 0, :], -1.0 / D, None, ALU.mult).then_inc(chain, 1)
                dve.wait_ge(chain, c0 + 4)
                dve.tensor_tensor(cen[:, :, :], x1, wide(stat[:, 1, :], TB), ALU.add).then_inc(chain, 1)
                dve.wait_ge(chain, c0 + 5)
                dve.tensor_tensor(tmp[:, :, :], cen[:, :, :], cen[:, :, :], ALU.mult).then_inc(chain, 1)
                dve.wait_ge(chain, c0 + 6)
                dve.tensor_reduce(stat[:, 2, :], tmp[:, :, :], AX.X, ALU.add).then_inc(var_done, 1)

            def scale_h1(s):
                dve.wait_ge(std_done, s + 1)
                dve.reciprocal(rstd[:, :], stat[:, 3, :]).then_inc(h1_done, 1)
                dve.wait_ge(h1_done, 2 * s + 1)
                dve.tensor_tensor(h1[:, :, :], cen[:, :, :], wide(rstd[:, :], TB), ALU.mult).then_inc(h1_done, 1)

            def strip(s):
                dve.wait_ge(runmax_done, s)
                for c in range(NC):
                    fold_chunk(s, c)
                    if c == 3:
                        search_classes(s - 1)
                        residual(s - 1)
                    if c == 4:
                        scale_h1(s - 1)
                    if c == 6:
                        search_candidates(s - 1)
                dve.wait_ge(runmax_turned, s)
                fold_maxima(s)

            for g in range(NC + 1):
                if g < NC:
                    centre(g)
                if g >= 1:
                    normalise(g - 1)
                if g >= 2:
                    fold_chunk(0, g - 2)
                if g < NC:
                    variance(g)
            constants()
            fold_chunk(0, NC - 1)
            fold_maxima(0)
            dve.wait_ge(x_b2_done, 1)
            with dve.Fori(1, S) as s:
                strip(s)
            residual(S - 1)
            scale_h1(S - 1)
            search_classes(S - 1)
            search_candidates(S - 1)

            dve.wait_ge(top_kept, 2 * S)
            dve.tensor_scalar(gap[:, 1, :], first[:, :], -1.0, MASK, ALU.add, ALU.mult).then_inc(end_chain, 1)
            dve.tensor_scalar(gap[:, 2, :], second[:, :], -1.0, MASK, ALU.add, ALU.mult).then_inc(end_chain, 1)
            dve.wait_ge(end_chain, 2)
            dve.tensor_tensor(gap[:, 3, :], gap[:, 1, :], gap[:, 2, :], ALU.subtract).then_inc(end_chain, 1)
            dve.wait_ge(end_chain, 3)
            dve.tensor_reduce(good[:, 0:1], gap[:, 3, :], AX.X, ALU.min).then_inc(end_chain, 1)
            dve.wait_ge(feat_done, S)
            dve.tensor_reduce(good[:, 1:2], feats_v[:, :, D:FA], AX.XY, ALU.max, apply_absolute_value=True)\
                .then_inc(end_chain, 1)
            dve.wait_ge(end_chain, 5)
            dve.tensor_scalar(good[:, 2:3], good[:, 0:1], LEAD, None, ALU.is_ge).then_inc(end_chain, 1)
            dve.wait_ge(end_chain, 6)
            dve.scalar_tensor_tensor(good[:, 3:4], good[:, 1:2], HALF_SCORE, good[:, 2:3], ALU.is_le, ALU.mult)\
                .then_inc(good_done, 1)
            dve.wait_ge(good_count, 1)
            dve.tensor_scalar(flag[:, :], ps_hid[0:1, 0:1], P - 0.5, None, ALU.is_lt).then_inc(flag_done, 1)

            for g in range(QG):
                ts = slice(g * OG, (g + 1) * OG)
                dve.wait_ge(got[g], 16 * OG)
                dve.tensor_tensor(gathered[:, ts, :], gathered[:, ts, :],
                                  bias_row[:, :].unsqueeze(1).to_broadcast([P, OG, D]), ALU.add).then_inc(biased, 1)
                dve.wait_ge(biased, g + 1)
                dve.scalar_tensor_tensor(gathered[:, ts, :].rearrange("q t d -> q (t d)"),
                                         gathered[:, ts, :].rearrange("q t d -> q (t d)"), 0.0,
                                         x_tq[:, ts, :].rearrange("q t d -> q (t d)"),
                                         ALU.max, ALU.add).then_inc(out_done, 1)

            dve.wait_ge(flag_done, 1)
            general = dve.value_load(flag[0:1, 0:1], min_val=0, max_val=1)
            with dve.If(general != 0):
                row, neigh, sc = ring[:, 0:N], ring[:, N:2 * N], h_t[:, :]
                for g in range(NB // 4):
                    dve.wait_ge(gen_turned, g + 1)
                    dve.tensor_copy(h_t[0:HEADS, g * W:(g + 1) * W].rearrange("h (q k) -> h k q", k=TB),
                                    acc[g % 2][0:HEADS, :].rearrange("h (k q) -> h k q", k=TB)).then_inc(gen_copied, 1)
                dve.wait_ge(out_done, QG)
                dve.wait_ge(stored, 16 * QG)
                dve.sem_inc(gen_head, 1)
                with dve.Fori(0, NB) as ib:
                    dve.wait_ge(gen_row_in, ib * 16 + 16)
                    dve.tensor_scalar(row, row, -1.0, MASK, ALU.add, ALU.mult).then_inc(gen_mask, 1)
                    with dve.Fori(0, HEADS) as h:
                        n = ib * HEADS + h
                        c0 = n * 7
                        dve.wait_ge(gen_neigh_in, n * 16 + 16)
                        dve.tensor_copy(gap[:, 3, 0:1], feats[:, bass.ds(ib * FA + D + h, 1)]).then_inc(gen_chain, 1)
                        dve.wait_ge(gen_chain, c0 + 1)
                        dve.tensor_scalar(sc, neigh, gap[:, 3, 0:1], None, ALU.add).then_inc(gen_chain, 1)
                        dve.wait_ge(gen_chain, c0 + 2)
                        dve.scalar_tensor_tensor(sc, sc, SLOPE, sc, ALU.mult, ALU.max).then_inc(gen_chain, 1)
                        dve.wait_ge(gen_chain, c0 + 3)
                        dve.wait_ge(gen_mask, ib * 2 + 1)
                        dve.tensor_tensor(sc, sc, row, ALU.add).then_inc(gen_chain, 1)
                        dve.wait_ge(gen_chain, c0 + 4)
                        dve.tensor_reduce(gap[:, 0, 0:1], sc, AX.X, ALU.max).then_inc(gen_chain, 1)
                        dve.wait_ge(gen_chain, c0 + 5)
                        dve.tensor_scalar(gap[:, 1, 0:1], gap[:, 0, 0:1], -1.0, None, ALU.mult).then_inc(gen_max, 1)
                        for g in range(NB // 4):
                            dve.wait_ge(gen_p_turned, n * (NB // 4) + g + 1)
                            dve.tensor_copy(max_lo[:, (g % 2) * W:(g % 2 + 1) * W], acc[g % 2][:, :])\
                                .then_inc(gen_p_copied, 1)
                        dve.wait_ge(gen_exp, n + 1)
                        dve.reciprocal(gap[:, 3, 1:2], gap[:, 2, 0:1]).then_inc(gen_chain, 1)
                        dve.wait_ge(gen_chain, c0 + 6)
                        dve.wait_ge(gen_sum, n + 1)
                        dve.tensor_scalar(cen[:, 0:1, :].rearrange("q a d -> q (a d)")[:, bass.ds(h * HD, HD)],
                                          ps_hid[:, 0:HD], gap[:, 3, 1:2], None, ALU.mult).then_inc(gen_chain, 1)
                        dve.wait_ge(gen_chain, c0 + 7)
                        dve.sem_inc(gen_head, 1)
                    dve.tensor_tensor(h1[:, 0, :], cen[:, 0, :], bias_row[:, :], ALU.add).then_inc(gen_mask, 1)
                    dve.wait_ge(gen_mask, ib * 2 + 2)
                    dve.scalar_tensor_tensor(tmp[:, 0, :], h1[:, 0, :], 0.0,
                                             x_tq[:, bass.ds(ib, 1), :].rearrange("q a d -> q (a d)"),
                                             ALU.max, ALU.add).then_inc(gen_out, 1)

        @block.tensor
        def _(pe):
            def turn_first(g):
                pe.wait_ge(pro_norm, g + 1)
                if g:
                    pe.wait_ge(pro_h, 2 * g)
                for k in range(CB):
                    last = pe.transpose(pro_banks[k // 4][:, k % 4, :], x_pb[:, g * CB + k, :], ident[:, :])
                last.then_inc(pro_turned, 1)

            def products(s, c, parity):
                pe.wait_ge(chunk_in[c % RING], s * (16 * NC // RING) + 16 * (c // RING + 1))
                for b in range(CB):
                    at = (b % 2) * D
                    last = pe.matmul(acc[parity][at:at + D, :], x_pb[:, c * CB + b, :], slot(c)[:, b * W:(b + 1) * W],
                                     start=(c == 0 and b < 2), stop=(c == NC - 1 and b >= CB - 2))
                return last

            def sums(c):
                for b in range(CB):
                    at = (b % 4) * QUAD
                    last = pe.matmul(row_sums[at:at + QUAD, :], ones_cols[:, :], slot(c)[:, b * W:(b + 1) * W],
                                     start=(c == 0 and b < 4), stop=(c == NC - 1 and b >= CB - 4))
                return last

            def chunk(s, c, parity, first=False):
                if c % 2:
                    pe.wait_ge(chunk_in[c % RING], s * (16 * NC // RING) + 16 * (c // RING + 1))
                    sums(c)
                last = products(s, c, parity)
                if c % 2 == 0:
                    if c == 0 and not first:
                        pe.wait_ge(rows_copied, s)
                    last = sums(c)
                last.then_inc(pe_chunk, 1)

            def mlp_hidden(s):
                pe.wait_ge(strip_h_done, 2 * s + 2)
                for k in range(2):
                    last = pe.matmul(ps_hid[:, k * (W // 2):(k + 1) * (W // 2)], w1_sb[:, k * HID:(k + 1) * HID],
                                     h_strip[:, :], start=True, stop=True)
                last.then_inc(hid_ready, 1)

            def turn_sums(s):
                pe.wait_ge(rows_copied, s + 1)
                pe.wait_ge(acc_copied, s + 1)
                pe.wait_ge(hid_done, s + 1)
                halves = [(k, slice(half, half + D), slice(k * P + half, k * P + half + D))
                          for k in range(TB) for half in (0, D)]
                for k, to, at in halves:
                    pe.matmul(ps_acc[to, k, D:2 * D], row_sb[:, at], fold_rows[:, :], start=True, stop=True)
                for k in range(TB):
                    for _, to, at in halves[2 * k:2 * k + 2]:
                        pe.matmul(ps_acc[to, k, 0:D], acc_sb[:, at], b_t_twice[:, :], start=True, stop=False)
                    for _, to, at in halves[2 * k:2 * k + 2]:
                        pe.matmul(ps_acc[to, k, 0:D], hidden[:, at], w2_sb[:, :], start=False, stop=True)
                for m in range(2):
                    last = pe.matmul(ps_xb[:, :, :].rearrange("q (h m) d -> q m h d", m=2)[:, m],
                                     h_strip[:, m * P:(m + 1) * P], b_t_diag[:, :], start=True, stop=True)
                last.then_inc(acc_turned, 1)

            def turn_maxima(s):
                pe.wait_ge(runmax_done, s + 1)
                for k in range(TB):
                    last = pe.transpose(ps_turn[:, k * P:(k + 1) * P], runmax[:, k * P:(k + 1) * P], ident[:, :])
                last.then_inc(runmax_turned, 1)

            def turn_h1(s, bank):
                pe.wait_ge(h1_done, 2 * s + 2)
                pe.sem_inc(pe_past, 1)
                for m in range(2):
                    last = pe.transpose(bank[:, m * P:(m + 1) * P],
                                        h1[:, 2 * m:2 * m + 2, :].rearrange("q t d -> q (t d)"), ident[:, :])
                last.then_inc(h1_turned, 1)

            def features(s):
                pe.wait_ge(h1_t_done, s + 1)
                for m in range(2):
                    last = pe.matmul(ps_feat[:, 2 * m:2 * m + 2, :].rearrange("q t f -> q (t f)"),
                                     h1_t[:, m * P:(m + 1) * P], w_ext[:, :], start=True, stop=True)
                last.then_inc(feat_ready, 1)

            def strip(s, parity):
                for c in range(NC):
                    if c == 1:
                        turn_maxima(s - 1)
                        turn_sums(s - 1)
                    chunk(s, c, parity)
                    if c == 4:
                        turn_h1(s - 1, ps_turn)
                    if c == 5:
                        features(s - 1)
                        mlp_hidden(s)

            for c in range(NC):
                pe.wait_ge(pro_norm, c + 1)
                chunk(0, c, 0, first=True)
                if c == 0:
                    pe.wait_ge(pool_const, 12)
                turn_first(c)
            pe.wait_ge(dve_const, 2)
            for k in range(2):
                last = pe.matmul(ps_feat[k * D:(k + 1) * D, 0, 0:2 * HEADS], w_gat_t_sb[:, :], att_diag[:, :],
                                 start=True, stop=True)
            last.then_inc(w_ext_ready, 1)
            pe.wait_ge(dve_const, 6)
            pe.wait_ge(w_ext_done, 2)
            mlp_hidden(0)
            with pe.Fori(0, S // 2 - 1) as r:
                strip(2 * r + 1, 1)
                strip(2 * r + 2, 0)
            strip(S - 1, 1)
            turn_maxima(S - 1)
            turn_sums(S - 1)
            turn_h1(S - 1, ps_hid)
            features(S - 1)
            pe.wait_ge(good_done, 1)
            pe.matmul(ps_hid[0:1, 0:1], good[:, 3:4], ones[:, :], start=True, stop=True).then_inc(good_count, 1)

            pe.wait_ge(flag_done, 1)
            general = pe.value_load(flag[0:1, 0:1], min_val=0, max_val=1)
            with pe.If(general != 0):
                for g in range(NB // 4):
                    if g >= 2:
                        pe.wait_ge(gen_copied, g - 1)
                    for k in range(4):
                        last = pe.transpose(acc[g % 2][0:HEADS, k * P:(k + 1) * P],
                                            feats_v[:, g * 4 + k, D + HEADS:FA], ident[:, :])
                    last.then_inc(gen_turned, 1)
                with pe.Fori(0, NB) as ib:
                    with pe.Fori(0, HEADS) as h:
                        n = ib * HEADS + h

                        def turn(g):
                            if g >= 2:
                                pe.wait_ge(gen_p_copied, n * (NB // 4) + g - 1)
                            neighbours = h_t[:, g * W:(g + 1) * W].rearrange("p (q k) -> p k q", k=TB)
                            for k in range(4):
                                last = pe.transpose(acc[g % 2][:, k * P:(k + 1) * P], neighbours[:, k], ident[:, :])
                            last.then_inc(gen_p_turned, 1)

                        pe.wait_ge(gen_exp, n + 1)
                        turn(0)
                        for g in range(NB // 4):
                            if g + 1 < NB // 4:
                                turn(g + 1)
                            pe.wait_ge(gen_p_copied, n * (NB // 4) + g + 1)
                            for k in range(4):
                                j = g * 4 + k
                                at = (g % 2) * W + k * P
                                last = pe.matmul(ps_hid[:, 0:HD], max_lo[:, at:at + P],
                                                 feats[:, bass.ds(h * HD + j * FA, HD)],
                                                 start=(j == 0), stop=(j == NB - 1))
                        last.then_inc(gen_sum, 1)


def kernel(x, adj, L0_gnn_t, L0_gnn_B, L0_gnn_W1, L0_gnn_b1, L0_gnn_W2, L0_gnn_b2,
           L1_gnn_W, L1_gnn_att_self, L1_gnn_att_neigh, L1_gnn_bias):
    import numpy as np
    import concourse.bacc as bacc
    from concourse.bass_utils import run_bass_kernel_spmd

    adj = np.asarray(adj)
    w1 = np.asarray(L0_gnn_W1)
    w_gat = np.asarray(L1_gnn_W)
    tiles = adj.reshape(S, P, TB, P, NC, CB).transpose(0, 4, 3, 5, 2, 1)
    arrays = {
        "x": x,
        "adj": adj,
        "adj_t": tiles.reshape(S * NC, P, CB * W),
        "w1": w1[0:D],
        "w1_t": w1[D:D + 1].reshape(HID, 1),
        "b1": np.asarray(L0_gnn_b1).reshape(HID, 1),
        "t_in": np.asarray(L0_gnn_t).reshape(1, 1),
        "w2": L0_gnn_W2,
        "b2": np.asarray(L0_gnn_b2).reshape(1, D),
        "b_t": np.asarray(L0_gnn_B).T,
        "w_gat": w_gat,
        "w_gat_t": w_gat.T,
        "att_self": np.asarray(L1_gnn_att_self).reshape(D, 1),
        "att_neigh": np.asarray(L1_gnn_att_neigh).reshape(D, 1),
        "bias": np.asarray(L1_gnn_bias).reshape(1, D),
    }
    nc = bacc.Bacc("TRN2", target_bir_lowering=False, num_devices=1)
    arrays = {f"in_{n}": np.ascontiguousarray(a) for n, a in arrays.items()}
    ins = [nc.dram_tensor(n, a.shape, mybir.dt.from_np(a.dtype), kind="ExternalInput").ap() for n, a in arrays.items()]
    out = nc.dram_tensor("out", (N, D), F32, kind="ExternalOutput").ap()
    build(nc, *ins, out)
    r = run_bass_kernel_spmd(nc, [arrays], core_ids=[0])
    return r.results[0]["out"]
```
